# Optimizing a Trainium2 kernel written in Bass

```python
import numpy as np
import jax
import jax.numpy as jnp

def _softmax(x, axis=-1):
    return jax.nn.softmax(x, axis=axis)

def _gelu(x):
    return jax.nn.gelu(x, approximate=True)

def _silu(x):
    return jax.nn.silu(x)

def _sigmoid(x):
    return jax.nn.sigmoid(x)

def _layernorm(x, axis=-1, eps=1e-05):
    m = jnp.mean(x, axis=axis, keepdims=True)
    v = jnp.var(x, axis=axis, keepdims=True)
    return (x - m) / jnp.sqrt(v + eps)

def _scatter_add(tgt, idx, src, axis=0):
    return tgt.at[idx].add(src)

def _segment_sum(src, seg, n):
    return jax.ops.segment_sum(src, seg, n)
kernel_name = 'mk_decoder_preln_d1_seqx_r8_98e815'

def setup_inputs(seed: int=0):
    np.random.seed(seed)
    _w = jnp.asarray

    def _rec_inputs():
        import jax
        import jax.numpy as jnp
        _rk = jax.random.key(seed)
        x = 7.22e-05 + 1 * jax.random.normal(jax.random.fold_in(_rk, 1), (32, 128, 128), jnp.float32)
        _lenS = 128 - jax.random.randint(jax.random.fold_in(_rk, 7), (32,), 0, max(1, 128 // 4) + 1, jnp.int32)
        _lenS2 = 128 - jax.random.randint(jax.random.fold_in(_rk, 8), (32,), 0, max(1, 128 // 4) + 1, jnp.int32)
        _ctx_1024P = jax.random.normal(jax.random.fold_in(_rk, 11), (32, 16, 128), jnp.float32)
        _ctx_1024c = jax.random.dirichlet(jax.random.fold_in(_rk, 511), 0.3 * jnp.ones((16,), jnp.float32), (32, 128))
        _ctx_1024t = jnp.einsum('bsk,bkd->bsd', _ctx_1024c, _ctx_1024P)
        _ctx_1024t = _ctx_1024t * jax.lax.rsqrt(jnp.mean(jnp.square(_ctx_1024t)) + 1e-12) * 0.953939
        ctx_1024 = 4.13588e-05 + 0.999923 * (_ctx_1024t + 0.3 * jax.random.normal(jax.random.fold_in(_rk, 611), (32, 128, 128), jnp.float32))
        return (x, ctx_1024)
    x, ctx_1024 = _rec_inputs()

    def _L0_attn_setup():
        import jax, jax.numpy as jnp
        import numpy as np
        OUT_DIM = 128
        key = jax.random.key(seed)
        k1, k2, k3, k4 = jax.random.split(key, 4)
        B, N, D = (4, 256, 128)
        s = 1.0 / np.sqrt(D)
        return {'x': jax.random.normal(k1, (B, N, D), dtype=jnp.float32), 'W_query': jax.random.normal(k2, (D, OUT_DIM), dtype=jnp.float32) * s, 'W_key': jax.random.normal(k3, (D, OUT_DIM), dtype=jnp.float32) * s, 'W_value': jax.random.normal(k4, (D, OUT_DIM), dtype=jnp.float32) * s}
    _L0_attn_all = _L0_attn_setup()
    _L0_attn_in = {k: v for k, v in _L0_attn_all.items() if k in ('W_query', 'W_key', 'W_value')}
    del _L0_attn_all

    def _L0_xattn_setup():
        import jax, jax.numpy as jnp
        import numpy as np
        D_MODEL = 128
        N_HEAD = 16
        D_HEAD = D_MODEL // N_HEAD
        NEG = -1000000000.0
        key = jax.random.key(seed)
        ks = jax.random.split(key, 11)
        B, T, C = (4, 256, D_MODEL)
        s = 1.0 / np.sqrt(C)
        return {'q': jax.random.normal(ks[0], (B, T, C), jnp.float32), 'k': jax.random.normal(ks[1], (B, T, C), jnp.float32), 'v': jax.random.normal(ks[2], (B, T, C), jnp.float32), 'w_q': jax.random.normal(ks[3], (C, C), jnp.float32) * s, 'b_q': jnp.zeros((C,), jnp.float32), 'w_k': jax.random.normal(ks[4], (C, C), jnp.float32) * s, 'b_k': jnp.zeros((C,), jnp.float32), 'w_v': jax.random.normal(ks[5], (C, C), jnp.float32) * s, 'b_v': jnp.zeros((C,), jnp.float32), 'w_o': jax.random.normal(ks[6], (C, C), jnp.float32) * s, 'b_o': jnp.zeros((C,), jnp.float32)}
    _L0_xattn_all = _L0_xattn_setup()
    _L0_xattn_in = {k: v for k, v in _L0_xattn_all.items() if k in ('w_q', 'b_q', 'w_k', 'b_k', 'w_v', 'b_v', 'w_o', 'b_o')}
    del _L0_xattn_all

    def _L0_ffn_setup():
        import jax, jax.numpy as jnp
        import numpy as np
        TEMPERATURE = 1.0
        TOPK = 2
        key = jax.random.key(seed)
        ks = jax.random.split(key, 6)
        S, B, H, F, E = (256, 4, 128, 512, 8)
        x = jax.random.normal(ks[0], (S, B, H), dtype=jnp.float32)
        gate_w = jax.random.normal(ks[1], (E, H), dtype=jnp.float32) * (1.0 / np.sqrt(H))
        w1 = jax.random.normal(ks[2], (E, H, F), dtype=jnp.float32) * (1.0 / np.sqrt(H))
        b1 = jnp.zeros((E, F), dtype=jnp.float32)
        w2 = jax.random.normal(ks[3], (E, F, H), dtype=jnp.float32) * (1.0 / np.sqrt(F))
        b2 = jnp.zeros((E, H), dtype=jnp.float32)
        return {'x': x, 'gate_w': gate_w, 'w1': w1, 'b1': b1, 'w2': w2, 'b2': b2}
    _L0_ffn_all = _L0_ffn_setup()
    _L0_ffn_in = {k: v for k, v in _L0_ffn_all.items() if k in ('gate_w', 'w1', 'b1', 'w2', 'b2')}
    del _L0_ffn_all
    return {'x': x, 'ctx_1024': ctx_1024, 'L0_attn_W_query': _L0_attn_in['W_query'], 'L0_attn_W_key': _L0_attn_in['W_key'], 'L0_attn_W_value': _L0_attn_in['W_value'], 'L0_xattn_w_q': _L0_xattn_in['w_q'], 'L0_xattn_b_q': _L0_xattn_in['b_q'], 'L0_xattn_w_k': _L0_xattn_in['w_k'], 'L0_xattn_b_k': _L0_xattn_in['b_k'], 'L0_xattn_w_v': _L0_xattn_in['w_v'], 'L0_xattn_b_v': _L0_xattn_in['b_v'], 'L0_xattn_w_o': _L0_xattn_in['w_o'], 'L0_xattn_b_o': _L0_xattn_in['b_o'], 'L0_ffn_gate_w': _L0_ffn_in['gate_w'], 'L0_ffn_w1': _L0_ffn_in['w1'], 'L0_ffn_b1': _L0_ffn_in['b1'], 'L0_ffn_w2': _L0_ffn_in['w2'], 'L0_ffn_b2': _L0_ffn_in['b2']}

def reference(x, ctx_1024, L0_attn_W_query, L0_attn_W_key, L0_attn_W_value, L0_xattn_w_q, L0_xattn_b_q, L0_xattn_w_k, L0_xattn_b_k, L0_xattn_w_v, L0_xattn_b_v, L0_xattn_w_o, L0_xattn_b_o, L0_ffn_gate_w, L0_ffn_w1, L0_ffn_b1, L0_ffn_w2, L0_ffn_b2):
    import jax
    import jax.numpy as jnp

    def _L0_attn_ref(x, W_query, W_key, W_value):
        import jax, jax.numpy as jnp
        import numpy as np
        OUT_DIM = 128
        q = jnp.einsum('bnd,de->bne', x, W_query)
        k = jnp.einsum('bnd,de->bne', x, W_key)
        v = jnp.einsum('bnd,de->bne', x, W_value)
        sqrt_d = jnp.sqrt(jnp.asarray(OUT_DIM, dtype=jnp.float32))
        scores = jnp.einsum('bie,bje->bij', q, k) / sqrt_d
        attn = jax.nn.softmax(scores, axis=1)
        return jnp.einsum('bij,bie->bje', attn, v)

    def _L0_xattn_ref(q, k, v, w_q, b_q, w_k, b_k, w_v, b_v, w_o, b_o):
        import jax, jax.numpy as jnp
        import numpy as np
        D_MODEL = 128
        N_HEAD = 16
        D_HEAD = D_MODEL // N_HEAD
        NEG = -1000000000.0
        B, T, C = q.shape
        qh = (q @ w_q + b_q).reshape(B, T, N_HEAD, D_HEAD).transpose(0, 2, 1, 3)
        kh = (k @ w_k + b_k).reshape(B, T, N_HEAD, D_HEAD).transpose(0, 2, 1, 3)
        vh = (v @ w_v + b_v).reshape(B, T, N_HEAD, D_HEAD).transpose(0, 2, 1, 3)
        scores = jnp.einsum('bhqd,bhkd->bhqk', qh, kh) / jnp.sqrt(jnp.asarray(D_HEAD, qh.dtype))
        causal = jnp.tril(jnp.ones((T, T), dtype=bool))
        scores = jnp.where(causal[None, None], scores, NEG)
        attn = jax.nn.softmax(scores, axis=-1)
        out = jnp.einsum('bhqk,bhkd->bhqd', attn, vh)
        out = out.transpose(0, 2, 1, 3).reshape(B, T, C)
        return out @ w_o + b_o

    def _L0_ffn_ref(x, gate_w, w1, b1, w2, b2):
        import jax, jax.numpy as jnp
        import numpy as np
        TEMPERATURE = 1.0
        TOPK = 2
        s, b, h = x.shape
        x_flat = x.reshape(s * b, h)
        logits = x_flat @ gate_w.T
        probs = jax.nn.softmax(logits / TEMPERATURE, axis=-1)
        topk_probs, topk_idx = jax.lax.top_k(probs, TOPK)
        hidden = jax.nn.relu(jnp.einsum('th,ehf->tef', x_flat, w1) + b1[None])
        all_out = jnp.einsum('tef,efh->teh', hidden, w2) + b2[None]
        gathered = jnp.take_along_axis(all_out, topk_idx[:, :, None], axis=1)
        y_flat = jnp.sum(gathered * topk_probs[:, :, None], axis=1)
        return y_flat.reshape(s, b, h)
    x = x + _L0_attn_ref(_layernorm(x, axis=-1), L0_attn_W_query, L0_attn_W_key, L0_attn_W_value)
    x = x + _L0_xattn_ref(_layernorm(x, axis=-1), ctx_1024, ctx_1024, L0_xattn_w_q, L0_xattn_b_q, L0_xattn_w_k, L0_xattn_b_k, L0_xattn_w_v, L0_xattn_b_v, L0_xattn_w_o, L0_xattn_b_o)
    x = x + _L0_ffn_ref(_layernorm(x, axis=-1), L0_ffn_gate_w, L0_ffn_w1, L0_ffn_b1, L0_ffn_w2, L0_ffn_b2)
    return x

_drawn_inputs = setup_inputs


def setup_inputs(seed=0):
    import zlib

    import numpy as np

    out = dict(_drawn_inputs(seed))
    spreads = {'L0_xattn_b_q': (0.0, 0.1),
     'L0_xattn_b_k': (0.0, 0.8),
     'L0_xattn_b_v': (0.0, 0.1),
     'L0_xattn_b_o': (0.0, 0.1),
     'L0_ffn_b1': (0.0, 0.312),
     'L0_ffn_b2': (0.0, 0.1)}
    factors = {}
    for name, (base, spread) in spreads.items():
        noise = np.random.default_rng([zlib.crc32(name.encode()), seed]).standard_normal(out[name].shape)
        drawn = base * np.exp(spread * noise) if base else spread * noise
        out[name] = jnp.asarray(drawn.astype(out[name].dtype))
    for name, factor in factors.items():
        out[name] = (out[name] * factor).astype(out[name].dtype)
    return out
```

```python
from contextlib import ExitStack

import concourse.bass as bass
from concourse import mybir

F32 = mybir.dt.float32
F32R = mybir.dt.float32r
BF16 = mybir.dt.bfloat16
U32 = mybir.dt.uint32
ALU = mybir.AluOpType
ACT = mybir.ActivationFunctionType
AX_X = mybir.AxisListType.X

P = 128
NB = 4
TOK = NB * P
HEADS = 16
DH = P // HEADS
GROUPS = 4
HPG = HEADS // GROUPS
UNITS = NB * GROUPS
EXPERTS = 8
KF = 4
STEPS = EXPERTS * KF
LAG = 2
AHEAD = 5
MASKED = -1e30
EPS = 1e-5
A_STEPS = 14


def wait(eng, sem, value):
    if not isinstance(value, int) or value > 0:
        eng.wait_ge(sem, value)


def before(p, n, ring):
    return STEPS * p + max(n - ring + 1, 0)


def decoder_layer(nc, x, ctx_in, Wq_s, Wk_s, Wv_s, w_q, b_q, w_k, b_k, w_v, b_v, w_o, b_o,
                  gate_w, w1, b1, w2, b2, out):
    B = x.shape[0]
    CHUNKS = B // NB
    SCALE_S = float(P) ** -0.5
    SCALE_X = float(DH) ** -0.5
    x_v = x.rearrange("(c b) p d -> c p b d", b=NB)
    ctx_v = ctx_in.rearrange("(c b) p d -> c p b d", b=NB)
    out_v = out.rearrange("(c b) p d -> c p b d", b=NB)

    with ExitStack() as stack:
        def sb(name, shape, dt=F32):
            return stack.enter_context(nc.sbuf_tensor(name, shape, dt))

        def sem(name):
            return stack.enter_context(nc.semaphore(name))

        identf = sb("identf", [P, P])
        identb = sb("identb", [P, P], BF16)
        maskb = sb("maskb", [P, P], BF16)
        head_rows = sb("head_rows", [P, HEADS], BF16)
        expert_rows = sb("expert_rows", [P, EXPERTS], F32R)
        q_hi_sel = sb("q_hi_sel", [P, GROUPS, P], F32R)
        q_lo_sel = sb("q_lo_sel", [P, GROUPS, P], F32R)
        k_hi_sel = sb("k_hi_sel", [P, GROUPS, P], F32R)
        k_lo_sel = sb("k_lo_sel", [P, GROUPS, P], F32R)
        minus_half = sb("minus_half", [P, NB])
        expert_no = sb("expert_no", [P, EXPERTS])
        Aqk = sb("Aqk", [P, P])
        wvs = sb("wvs", [P, P])
        wqx = sb("wqx", [P, P])
        wkx = sb("wkx", [P, P])
        wvx = sb("wvx", [P, P])
        wo = sb("wo", [P, 2, P])
        gw = sb("gw", [P, EXPERTS])
        cols = sb("cols", [P, 64])
        bv = sb("bv", [P, P])
        bo = sb("bo", [P, P])
        w1_hi = sb("w1_hi", [P, EXPERTS, TOK], F32R)
        w1_lo = sb("w1_lo", [P, EXPERTS, TOK], F32R)
        w2_hi = sb("w2_hi", [P, EXPERTS, KF, P], F32R)
        w2_lo = sb("w2_lo", [P, EXPERTS, KF, P], F32R)
        B1, B2, GW, BQ, BK = 0, STEPS, STEPS + 8, STEPS + 16, STEPS + 17
        X = sb("X", [P, NB, P])
        C = sb("C", [P, NB, P])
        xn = sb("xn", [P, NB, P])
        PTs = xn
        xnT = sb("xnT", [P, TOK])
        cT = sb("cT", [P, TOK])
        x3T = cT
        Vs = C
        PT = sb("PT", [P, 2, TOK])
        Ps, GT = PT[:, 0, :], PT[:, 1, :]
        V4 = sb("V4", [P, NB, P])
        qk_hi = sb("qk_hi", [P, TOK], F32R)
        qk_lo = sb("qk_lo", [P, TOK], F32R)
        Kst = sb("Kst", [P, GROUPS, TOK], F32R)
        Qst = sb("Qst", [P, GROUPS, TOK], F32R)
        Kbd = sb("Kbd", [P, 2, GROUPS, HPG, P], F32R)
        Qbd = sb("Qbd", [P, 2, GROUPS, HPG, P], F32R)
        Vpad = sb("Vpad", [P, 2, HEADS, P])
        w_stage = Vpad[:, :, :, :].rearrange("p a h c -> p (a h c)").rearrange("p (e n) -> p e n", e=EXPERTS)
        smx = sb("smx", [P, NB])
        nmx = sb("nmx", [P, NB])
        sden = sb("sden", [P, NB])
        srden = sb("srden", [P, NB])
        mx = sb("mx", [P, 2, HEADS])
        mcol = sb("mcol", [P, P], BF16)
        mT = sb("mT", [P, 2, P], BF16)
        Osb = sb("Osb", [P, 2, P])
        Dsb = sb("Dsb", [P, 2, P])
        ON = sb("ON", [P, 2, P])
        x3n = sb("x3n", [P, P])
        st1 = sb("st1", [P, NB, 6])
        mv1 = sb("mv1", [P, NB, 2])
        ve1 = sb("ve1", [P, NB])
        rs1 = sb("rs1", [P, NB])
        st3 = sb("st3", [P, 6])
        mv3 = sb("mv3", [P, 2])
        ve3 = sb("ve3", [P, 1])
        rs3 = sb("rs3", [P, 1])
        x2 = sb("x2", [P, 2, NB, P])
        x3_hi = sb("x3_hi", [P, 2, TOK], F32R)
        x3_lo = sb("x3_lo", [P, 2, TOK], F32R)
        h_full = sb("h_full", [P, 2, TOK])
        h_hi = sb("h_hi", [P, 3, TOK], F32R)
        h_lo = sb("h_lo", [P, 3, TOK], F32R)
        Gb = sb("Gb", [P, 2, TOK])
        yt = sb("yt", [P, TOK])
        yacc = sb("yacc", [P, TOK])
        lg = sb("lg", [P, NB, EXPERTS])
        ex = sb("ex", [P, NB, EXPERTS])
        top = sb("top", [P, NB, 8])
        topi = sb("topi", [P, NB, 8], U32)
        topf = sb("topf", [P, NB, 8])
        is1 = sb("is1", [P, NB, EXPERTS])
        is2 = sb("is2", [P, NB, EXPERTS])
        gden = sb("gden", [P, NB])
        grden = sb("grden", [P, NB])
        gate = sb("gate", [P, NB, EXPERTS])
        gcol = sb("gcol", [P, NB, P])
        gT = sb("gT", [P, TOK], F32R)

        def pb(name):
            return stack.enter_context(nc.psum_tensor(name, [P, TOK], F32))

        pS, pT0, pT1, pO, pG, pH0, pH1, pY = (pb(n) for n in ("pS", "pT0", "pT1", "pO", "pG", "pH0", "pH1", "pY"))
        pT = (pT0, pT1)
        pH = (pH0, pH1)
        pG_b = pG[:, 0:P // 2].bitcast(BF16)

        zeroed, selected, rows_in, wts_in, w1_in, w2_in, wo_in = (
            sem(n) for n in ("zeroed", "selected", "rows_in", "wts_in", "w1_in", "w2_in", "wo_in"))
        cast_done, setup_T, setup_cp, aqk_ps, aqk_ready, w_hi, w_lo, vpad_init, sel_step = (
            sem(n) for n in ("cast_done", "setup_T", "setup_cp", "aqk_ps", "aqk_ready", "w_hi", "w_lo", "vpad_init", "sel_step"))
        x_in, c_in, out_done = sem("x_in"), sem("c_in"), sem("out_done")
        kbd_in = (sem("kbd_in0"), sem("kbd_in1"))
        qbd_in = (sem("qbd_in0"), sem("qbd_in1"))
        (ln_stat, ln_agg, ln_ve, ln_rstd, xn_ready, xT_ps, cT_ps, g_ps, vs_ps, k_ps, vx_ps, ss_ps, st_kps,
         xnT_ready, cT_ready, gt_ready, vs_ready, khi_ready, klo_ready, vx_ready, smax_done, nmx_ready, p_ready,
         kst_a, kst_d, pt_ps, pts_ready, pvs_ps, srden_done, x1_done, x1b_ready, q_ps, qst_ps, qst_a, qst_d) = (
            sem(n) for n in (
                "ln_stat", "ln_agg", "ln_ve", "ln_rstd", "xn_ready", "xT_ps", "cT_ps", "g_ps", "vs_ps", "k_ps",
                "vx_ps", "ss_ps", "kst_ps", "xnT_ready", "cT_ready", "gt_ready", "vs_ready", "qkhi_ready",
                "qklo_ready", "vx_ready", "smax_done", "nmx_ready", "p_ready", "kst_a", "kst_d", "pt_ps",
                "pts_ready", "pvs_ps", "srden_done", "x1_done", "x1b_ready", "q_ps", "qst_ps", "qst_a", "qst_d"))
        kst_ps, qkhi_ready, qklo_ready = st_kps, khi_ready, klo_ready
        (s_ps, max_done, m_hi, mcol_ready, mT_ps, mT_ready, st_ps, exp_done, keep_done, vpad_ready, pv_ps,
         o_evac, o_shuf, o_rec, on_ready, wo_ps, x2_done, st3_done, mv3_done, ve3_done, rs3_done, x3n_ready,
         x3T_ps, x3hi_ready, x3T_ready, x3_ready) = (
            sem(n) for n in (
                "s_ps", "max_done", "m_hi", "mcol_ready", "mT_ps", "mT_ready", "st_ps", "exp_done", "keep_done",
                "vpad_ready", "pv_ps", "o_evac", "o_shuf", "o_rec", "on_ready", "wo_ps", "x2_done", "st3_done",
                "mv3_done", "ve3_done", "rs3_done", "x3n_ready", "x3T_ps", "x3hi_ready", "x3T_ready", "x3_ready"))
        (lg_ps, lg_copied, top_done, topi_done, ex_in_done, ex_done, topf_done, gate_step, gcol_ready, gT_ps,
         gT_ready, gb_ps, gb_ready, up_ps, relu_done, lo_ready, dn_ps, y_scaled, y_added, oT_ps, out_ready) = (
            sem(n) for n in (
                "lg_ps", "lg_copied", "top_done", "topi_done", "ex_in_done", "ex_done", "topf_done", "gate_step",
                "gcol_ready", "gT_ps", "gT_ready", "gb_ps", "gb_ready", "up_ps", "relu_done", "lo_ready", "dn_ps",
                "y_scaled", "y_added", "oT_ps", "out_ready"))

        block = stack.enter_context(nc.Block())

        def wait_apart(eng, sem, value):
            if not isinstance(value, int):
                value = eng.to_reg(value)
                eng.wait_ge(selected, 1)
            wait(eng, sem, value)

        def cols_of(t, b):
            return t[:, b * P:(b + 1) * P]

        def tiles(t):
            return t[:, :].rearrange("p (b n) -> p b n", b=NB)

        @block.sync
        def _(sp):
            sp.dma_start(X[:, :, :], x_v[0]).then_inc(x_in, 16)
            sp.dma_start(C[:, :, :], ctx_v[0]).then_inc(c_in, 16)
            wts = ((h_full[:, 0, 0:P], Wq_s), (h_full[:, 0, P:2 * P], Wk_s), (wvs[:, :], Wv_s), (wqx[:, :], w_q),
                   (wkx[:, :], w_k), (wvx[:, :], w_v), (bv[:, :], b_v.partition_broadcast(P)),
                   (bo[:, :], b_o.partition_broadcast(P)))
            for dst, src in wts:
                sp.dma_start(dst, src).then_inc(wts_in, 16)
            sp.wait_ge(zeroed, 2)
            small = h_full[:, 0, 2 * P:3 * P]
            rows = ((B1, b1.rearrange("e (k p) -> (e k) p", p=P)), (B2, b2), (GW, gate_w),
                    (BQ, b_q.rearrange("(a n) -> a n", a=1)), (BK, b_k.rearrange("(a n) -> a n", a=1)))
            for r, src in rows:
                sp.dma_start(small[r:r + src.shape[0], :], src).then_inc(rows_in, 16)
            sp.dma_start(w_stage, w1.rearrange("e h f -> h e f")).then_inc(w1_in, 16)
            for h in range(HEADS):
                r = 2 * DH * (h % 8)
                sp.dma_start(wo[r:r + DH, h // 8, :], w_o[h * DH:(h + 1) * DH, :]).then_inc(wo_in, 16)
            sp.wait_ge(w_lo, EXPERTS)
            sp.dma_start(w_stage.rearrange("p e (k n) -> p e k n", k=KF),
                         w2.rearrange("e (k p) h -> p e k h", p=P)).then_inc(w2_in, 16)

            def spread(bd, st, slot, b, done):
                for j in range(HPG):
                    sp.dma_start(bd[32 * j:32 * j + 32, slot, :, j, :].bitcast(F32),
                                 st[32 * j:32 * j + 32, :, b * P:(b + 1) * P].bitcast(F32)).then_inc(done[slot], 16)

            def transfers(c, last, experts):
                wait_apart(sp, kst_a, 2 * c + 2)
                wait_apart(sp, kst_d, 2 * c + 2)
                wait_apart(sp, s_ps, UNITS * c)
                spread(Kbd, Kst, 0, 0, kbd_in)
                spread(Kbd, Kst, 1, 1, kbd_in)
                wait_apart(sp, pvs_ps, c + 1)
                if not last:
                    sp.dma_start(C[:, :, :], ctx_v[bass.ds(c + 1, 1)].rearrange("a p b d -> p (a b) d")).then_inc(c_in, 16)
                wait_apart(sp, qst_a, 2 * c + 2)
                wait_apart(sp, qst_d, 2 * c + 2)
                wait_apart(sp, st_ps, UNITS * c)
                spread(Qbd, Qst, 0, 0, qbd_in)
                spread(Qbd, Qst, 1, 1, qbd_in)
                wait_apart(sp, s_ps, UNITS * c + 4)
                spread(Kbd, Kst, 0, 2, kbd_in)
                wait_apart(sp, s_ps, UNITS * c + 8)
                spread(Kbd, Kst, 1, 3, kbd_in)
                wait_apart(sp, st_ps, UNITS * c + 4)
                spread(Qbd, Qst, 0, 2, qbd_in)
                wait_apart(sp, st_ps, UNITS * c + 8)
                spread(Qbd, Qst, 1, 3, qbd_in)
                if not last:
                    wait_apart(sp, x2_done, NB * c + NB)
                    sp.dma_start(X[:, :, :], x_v[bass.ds(c + 1, 1)].rearrange("a p b d -> p (a b) d")).then_inc(x_in, 16)
                if experts:
                    store(c - 1)

            def store(p):
                wait_apart(sp, out_ready, p + 1)
                src = x2[:, bass.ds(p % 2, 1), :, :].rearrange("p a b d -> p (a b) d")
                sp.dma_start(out_v[bass.ds(p, 1)].rearrange("a p b d -> p (a b) d"), src).then_inc(out_done, 16)

            transfers(0, False, False)
            transfers(1, False, True)
            with sp.Fori(2, CHUNKS - 1) as c:
                transfers(c, False, True)
            transfers(CHUNKS - 1, True, True)
            store(CHUNKS - 1)
            sp.wait_ge(out_done, 16 * CHUNKS)

        @block.gpsimd
        def _(pool):
            pool.memset(h_full[:, 0, 2 * P:3 * P], 0.0).then_inc(zeroed, 1)
            pool.memset(wo[:, :, :], 0.0).then_inc(zeroed, 1)
            pool.memset(identf[:, :], 0.0)
            pool.memset(maskb[:, :], 0.0)
            pool.memset(head_rows[:, :], 0.0)
            pool.memset(h_full[:, 1, 0:EXPERTS], 0.0)
            pool.memset(PT[:, :, :], 0.0)
            pool.memset(yacc[:, :], 0.0)
            pool.memset(V4[:, :, :], 0.0)
            pool.memset(minus_half[:, :], -0.5)
            for e in range(EXPERTS):
                pool.memset(expert_no[:, e:e + 1], float(e))
            pool.memset(gcol[:, :, :], 0.0)
            pool.memset(mcol[:, :], 0.0).then_inc(sel_step, 1)
            pool.wait_ge(sel_step, 1)
            pool.affine_select(out=identf[:, :], in_=identf[:, :], compare_op=ALU.not_equal, fill=1.0, base=0,
                               pattern=[[-1, P]], channel_multiplier=1)
            pool.affine_select(out=maskb[:, :], in_=maskb[:, :], compare_op=ALU.is_ge, fill=MASKED, base=0,
                               pattern=[[-1, P]], channel_multiplier=1)
            pick = ((PT[:, 0, :], slice(0, 2)), (PT[:, 1, :], slice(2, 4)),
                    (yacc[:, :], slice(0, 4, 2)),
                    (V4[:, :, :].rearrange("p b n -> p (b n)"), slice(1, 4, 2)))
            for t, copies in pick:
                v = t.rearrange("p (h i d) -> p h i d", h=HEADS, d=DH)[:, :, copies, :]
                pool.affine_select(out=v, in_=v, compare_op=ALU.not_equal, fill=1.0, base=0,
                                   pattern=[[-DH, HEADS], [0, 2], [-1, DH]], channel_multiplier=1)
            for base in (0, -HEADS):
                pool.affine_select(out=head_rows[:, :], in_=head_rows[:, :], compare_op=ALU.not_equal, fill=1.0,
                                   base=base, pattern=[[-1, HEADS]], channel_multiplier=1).then_inc(sel_step, 1)
                pool.wait_ge(sel_step, 2 if base == 0 else 3)
            for base in (0, -EXPERTS):
                v = h_full[:, 1, 0:EXPERTS]
                pool.affine_select(out=v, in_=v, compare_op=ALU.not_equal, fill=1.0, base=base,
                                   pattern=[[-1, EXPERTS]], channel_multiplier=1).then_inc(sel_step, 1)
                pool.wait_ge(sel_step, 4 if base == 0 else 5)
            pool.memset(Kbd[:, :, :, :, :].bitcast(F32), 0.0)
            pool.memset(Qbd[:, :, :, :, :].bitcast(F32), 0.0).then_inc(selected, 1)

            def power(ve, rs, n):
                return pool.tensor_tensor(rs, ve, minus_half[:, 0:n], ALU.pow)

            def fill_vpad(c, b):
                wait_apart(pool, pv_ps, UNITS * c + GROUPS * (b - 1))
                wait_apart(pool, vx_ready, c + 1)
                w = P + 2 * DH
                for half in range(2):
                    flat = Vpad[:, b % 2, 8 * half:8 * half + 8, :].rearrange("p h n -> p (h n)")
                    vals = V4[:, b, 64 * half:64 * half + 64].rearrange("p (h d) -> p h d", d=DH)
                    pool.tensor_copy(flat[:, 0:7 * w].rearrange("p (h n) -> p h n", n=w)[:, :, 0:DH], vals[:, 0:7, :])
                    ins = pool.tensor_copy(flat[:, 7 * w:7 * w + DH], vals[:, 7, :])
                ins.then_inc(vpad_ready, 1)

            def keep_causal(c, u):
                wait_apart(pool, exp_done, UNITS * c + u + 1)
                v = PT[:, u % 2, :].rearrange("p (h q) -> p h q", h=HPG)
                pool.affine_select(out=v, in_=v, compare_op=ALU.is_ge, fill=0.0, base=0,
                                   pattern=[[0, HPG], [1, P]], channel_multiplier=-1).then_inc(keep_done, 1)

            def expert_step(p, n):
                e, r = divmod(n - 6, KF)
                if r == 0 and 1 <= e < EXPERTS:
                    pool.wait_ge(y_scaled, EXPERTS * p + e + 1)
                    pool.tensor_tensor(yacc[:, :], yacc[:, :], yt[:, :], ALU.add).then_inc(y_added, 1)
                    pool.wait_ge(y_added, (EXPERTS - 1) * p + e)

            def third_power(c, b):
                pool.wait_ge(ve3_done, NB * c + b + 1)
                power(ve3[:, :], rs3[:, :], 1).then_inc(rs3_done, 1)

            def body(c, experts):
                p = c - 1
                pool.wait_ge(ln_ve, 2 * c + 1)
                power(ve1[:, :], rs1[:, :], NB).then_inc(ln_rstd, 1)
                for n in range(8):
                    if experts:
                        expert_step(p, n)
                pool.wait_ge(ln_ve, 2 * c + 2)
                power(ve1[:, :], rs1[:, :], NB).then_inc(ln_rstd, 1)
                if isinstance(c, int) and c == 0:
                    pool.wait_ge(vpad_init, 1)
                fill_vpad(c, 0)
                fill_vpad(c, 1)
                pool.wait_ge(xn_ready, 2 * c + 2)
                for b in range(NB):
                    ins = pool.tensor_tensor(X[:, b, :], X[:, b, :], bo[:, :], ALU.add)
                ins.then_inc(x1b_ready, 1)
                for n in range(8, A_STEPS):
                    if experts:
                        expert_step(p, n)
                for u in range(UNITS):
                    b, g = divmod(u, GROUPS)
                    keep_causal(c, u)
                    if g == 1 and 2 <= b + 1 < NB:
                        fill_vpad(c, b + 1)
                    if g == 2 and b >= 1:
                        third_power(c, b - 1)
                    if experts:
                        expert_step(p, A_STEPS + u)
                if experts:
                    expert_step(p, 30)
                third_power(c, NB - 1)
                if experts:
                    expert_step(p, 34)

            body(0, False)
            body(1, True)
            with pool.Fori(2, CHUNKS) as c:
                body(c, True)
            for n in range(STEPS + 3):
                expert_step(CHUNKS - 1, n)

        @block.scalar
        def _(act):
            def copy(dst, src):
                return act.activation(dst, src, ACT.Copy)

            def expert_step(p, n):
                if n < STEPS:
                    act.wait_ge(up_ps, STEPS * p + n + 1)
                    wait(act, dn_ps, before(p, n, 3))
                    act.activation(h_hi[:, n % 3, :], pH[n % 2][:, :], ACT.Relu, bias=cols[:, B1 + n:B1 + n + 1])
                    wait(act, lo_ready, before(p, n, 2))
                    act.activation(h_full[:, n % 2, :], pH[n % 2][:, :], ACT.Relu,
                                   bias=cols[:, B1 + n:B1 + n + 1]).then_inc(relu_done, 1)
                if n % KF == 2 and n < STEPS:
                    e = n // KF
                    act.wait_ge(gb_ps, EXPERTS * p + e + 1)
                    wait(act, y_scaled, EXPERTS * p + max(e - 1, 0))
                    copy(Gb[:, e % 2, :], pG[:, :]).then_inc(gb_ready, 1)

            def gates_T(p):
                act.wait_ge(gT_ps, p + 1)
                wait(act, gb_ps, EXPERTS * p)
                copy(gT[:, :], pG[:, :]).then_inc(gT_ready, 1)

            def stack_evac(dst, ps, done, c):
                for g in (0, 2):
                    act.wait_ge(ps, GROUPS * c + g + 1)
                    copy(dst[:, g, :], pT0[:, :]).then_inc(done, 1)
                    yield

            def third_T(c, b):
                act.wait_ge(x3T_ps, NB * c + b + 1)
                wait(act, oT_ps, c - 1)
                copy(x3_hi[:, bass.ds(c % 2, 1), b * P:(b + 1) * P].rearrange("p a n -> p (a n)"),
                     pG[:, 0:P]).then_inc(x3hi_ready, 1)

            def body(c, experts):
                p = c - 1

                def step(n):
                    if experts:
                        expert_step(p, n)

                act.wait_ge(xT_ps, 2 * c + 1)
                copy(xnT[:, :], pT0[:, :]).then_inc(xnT_ready, 1)
                step(0)
                act.wait_ge(g_ps, c + 1)
                copy(GT, pS[:, :]).then_inc(gt_ready, 1)
                if experts:
                    gates_T(p)
                step(1)
                act.wait_ge(k_ps, c + 1)
                wait(act, qst_ps, GROUPS * c)
                act.activation(qk_hi[:, :], pT0[:, :], ACT.Identity, bias=cols[:, BK:BK + 1]).then_inc(qkhi_ready, 1)
                step(2)
                step(3)
                for b in range(NB):
                    act.wait_ge(nmx_ready, c + 1)
                    ins = act.activation(cols_of(Ps, b), cols_of(pS, b), ACT.Exp, bias=nmx[:, b:b + 1],
                                         scale=SCALE_S, accum_out=sden[:, b:b + 1])
                ins.then_inc(p_ready, 1)
                step(4)
                kst = stack_evac(Kst, kst_ps, kst_a, c)
                wait(act, st_ps, UNITS * c)
                next(kst)
                step(5)
                next(kst)
                step(6)
                act.wait_ge(pt_ps, c + 1)
                copy(PTs[:, :, :].rearrange("p b n -> p (b n)"), pO[:, :]).then_inc(pts_ready, 1)
                step(7)
                step(8)
                step(9)
                act.wait_ge(xT_ps, 2 * c + 2)
                copy(xnT[:, :], pO[:, :]).then_inc(xnT_ready, 1)
                act.wait_ge(q_ps, c + 1)
                act.wait_ge(kst_ps, GROUPS * (c + 1))
                act.activation(qk_hi[:, :], pT0[:, :], ACT.Identity, bias=cols[:, BQ:BQ + 1]).then_inc(qkhi_ready, 1)
                step(10)
                qst = stack_evac(Qst, qst_ps, qst_a, c)
                wait(act, s_ps, UNITS * c)
                next(qst)
                step(11)
                next(qst)
                step(12)
                step(13)

                def m_T(b):
                    act.wait_ge(mT_ps, NB * c + b + 1)
                    wait(act, st_ps, UNITS * c + GROUPS * (b - 1))
                    copy(mT[:, b % 2, :], pG_b).then_inc(mT_ready, 1)

                def o_copy(b):
                    act.wait_ge(pv_ps, UNITS * c + GROUPS * (b + 1))
                    wait(act, on_ready, NB * c + b)
                    copy(Osb[:, :, :].rearrange("p a n -> p (a n)"), pO[:, 0:2 * P]).then_inc(o_evac, 1)

                m_T(0)
                for u in range(UNITS):
                    b, g = divmod(u, GROUPS)
                    act.wait_ge(st_ps, UNITS * c + u + 1)
                    wait(act, pv_ps, UNITS * c + u - 1)
                    act.activation(PT[:, u % 2, :], pT[u % 2][:, :], ACT.Exp, scale=SCALE_X).then_inc(exp_done, 1)
                    if g == 0 and b >= 1:
                        o_copy(b - 1)
                    if g == 0 and b >= 2:
                        third_T(c, b - 2)
                    step(A_STEPS + u)
                    if g == 3 and b + 1 < NB:
                        m_T(b + 1)
                o_copy(NB - 1)
                third_T(c, NB - 2)
                step(30)
                step(31)
                third_T(c, NB - 1)
                act.wait_ge(ex_in_done, c + 1)
                act.activation(ex[:, :, :], ex[:, :, :], ACT.Exp).then_inc(ex_done, 1)

            act.wait_ge(cast_done, 1)
            for t, src_in in ((w1_hi, w1_in), (w2_hi, w2_in)):
                act.wait_ge(src_in, 16)
                for e in range(EXPERTS):
                    dst = t[:, e] if t is w1_hi else t[:, e].rearrange("p k n -> p (k n)")
                    copy(dst, w_stage[:, e, :]).then_inc(w_hi, 1)
            act.wait_ge(aqk_ready, 1)
            body(0, False)
            body(1, True)
            with act.Fori(2, CHUNKS) as c:
                body(c, True)
            gates_T(CHUNKS - 1)
            for n in range(STEPS):
                expert_step(CHUNKS - 1, n)

        @block.vector
        def _(dve):
            dve.wait_ge(selected, 1)
            dve.tensor_copy(identb[:, :], identf[:, :])
            for t, src in ((q_hi_sel, PT[:, 0, :]), (q_lo_sel, PT[:, 1, :]),
                           (k_hi_sel, yacc[:, :]),
                           (k_lo_sel, V4[:, :, :].rearrange("p b n -> p (b n)"))):
                dve.tensor_copy(t[:, :, :].rearrange("p g n -> p (g n)"), src)
            dve.tensor_copy(expert_rows[:, :], h_full[:, 1, 0:EXPERTS]).then_inc(cast_done, 1)
            dve.wait_ge(setup_T, 1)
            dve.tensor_copy(h_full[:, 1, P:3 * P], pH0[:, 0:2 * P])
            dve.tensor_copy(cols[:, :], pH0[:, 2 * P:2 * P + 64])
            dve.tensor_copy(gw[:, :], pH0[:, 2 * P + GW:2 * P + GW + EXPERTS]).then_inc(setup_cp, 1)
            dve.wait_ge(aqk_ps, 1)
            dve.tensor_copy(Aqk[:, :], pH1[:, 0:P]).then_inc(aqk_ready, 1)
            i = 0
            for t, hi in ((w1_lo, w1_hi), (w2_lo, w2_hi)):
                for e in range(EXPERTS):
                    i += 1
                    dve.wait_ge(w_hi, i)
                    flat = (lambda a: a[:, e]) if t is w1_lo else (lambda a: a[:, e].rearrange("p k n -> p (k n)"))
                    dve.tensor_tensor(flat(t), w_stage[:, e, :], flat(hi).bitcast(F32), ALU.subtract).then_inc(w_lo, 1)
            dve.wait_ge(w_lo, 2 * EXPERTS)
            dve.memset(Vpad[:, :, :, :], 0.0).then_inc(setup_cp, 1)
            dve.wait_ge(setup_cp, 2)
            for s in range(2):
                for h in range(HEADS):
                    c0 = 2 * DH * (h % 8) + DH
                    ins = dve.memset(Vpad[:, s, h, c0:c0 + DH], 1.0)
            ins.then_inc(vpad_init, 1)

            def norm(src, dst, i, done):
                for b in range(NB):
                    ins = dve.bn_stats(st1[:, b, :], src[:, b, :])
                ins.then_inc(ln_stat, 1)
                wait_apart(dve, ln_stat, i)
                for b in range(NB):
                    ins = dve.bn_aggr(mv1[:, b, :], st1[:, b, :])
                ins.then_inc(ln_agg, 1)
                dve.wait_ge(ln_agg, i)
                dve.tensor_scalar(ve1[:, :], mv1[:, :, 1], EPS, None, ALU.add).then_inc(ln_ve, 1)
                dve.wait_ge(ln_rstd, i)
                for b in range(NB):
                    ins = dve.tensor_scalar(dst[:, b, :], src[:, b, :], mv1[:, b, 0:1], rs1[:, b:b + 1],
                                            ALU.subtract, ALU.mult)
                ins.then_inc(done, 1)

            def expert_scale(p, e):
                dve.wait_ge(dn_ps, STEPS * p + KF * (e + 1))
                dve.wait_ge(gb_ready, EXPERTS * p + e + 1)
                if e == 0:
                    wait(dve, oT_ps, p)
                else:
                    wait(dve, y_added, (EXPERTS - 1) * p + e - 1)
                dve.scalar_tensor_tensor(out=(yacc if e == 0 else yt)[:, :], in0=pY[:, :],
                                         scalar=cols[:, B2 + e:B2 + e + 1], in1=Gb[:, e % 2, :],
                                         op0=ALU.add, op1=ALU.mult).then_inc(y_scaled, 1)

            def expert_step(p, n):
                e, r = divmod(n - 6, KF)
                if r == 0 and e >= 0:
                    expert_scale(p, e)
                if n < STEPS:
                    dve.wait_ge(relu_done, STEPS * p + n + 1)
                    wait(dve, dn_ps, before(p, n, 3))
                    dve.tensor_tensor(h_lo[:, n % 3, :], h_full[:, n % 2, :], h_hi[:, n % 3, :].bitcast(F32),
                                      ALU.subtract).then_inc(lo_ready, 1)

            def out_add(p):
                dve.wait_ge(oT_ps, p + 1)
                v = x2[:, bass.ds(p % 2, 1), :, :].rearrange("p a b d -> p (a b d)")
                dve.tensor_tensor(v, pG[:, :], v, ALU.add).then_inc(out_ready, 1)

            def third_x2(c, b):
                v = x2[:, bass.ds(c % 2, 1), b, :].rearrange("p a d -> p (a d)")
                dve.wait_ge(wo_ps, NB * c + b + 1)
                dve.wait_ge(x1b_ready, c + 1)
                if b == 0:
                    wait(dve, out_done, 16 * (c - 1))
                dve.tensor_tensor(v, pG[:, 0:P], X[:, b, :], ALU.add).then_inc(x2_done, 1)
                wait_apart(dve, x2_done, NB * c + b + 1)
                dve.bn_stats(st3[:, :], v).then_inc(st3_done, 1)
                wait_apart(dve, st3_done, NB * c + b + 1)
                dve.bn_aggr(mv3[:, :], st3[:, :]).then_inc(mv3_done, 1)
                dve.wait_ge(mv3_done, NB * c + b + 1)
                dve.tensor_scalar(ve3[:, :], mv3[:, 1:2], EPS, None, ALU.add).then_inc(ve3_done, 1)

            def third_norm(c, b):
                dve.wait_ge(rs3_done, NB * c + b + 1)
                wait(dve, x3T_ps, NB * c + b)
                v = x2[:, bass.ds(c % 2, 1), b, :].rearrange("p a d -> p (a d)")
                dve.tensor_scalar(x3n[:, :], v, mv3[:, 0:1], rs3[:, :], ALU.subtract, ALU.mult).then_inc(x3n_ready, 1)

            def third_T(c, b):
                dve.wait_ge(x3T_ps, NB * c + b + 1)
                dve.wait_ge(x3hi_ready, NB * c + b + 1)
                dve.tensor_copy(x3T[:, b * P:(b + 1) * P], pG[:, 0:P]).then_inc(x3T_ready, 1)
                dve.wait_ge(x3T_ready, NB * c + b + 1)
                hi, lo = (t[:, bass.ds(c % 2, 1), b * P:(b + 1) * P].rearrange("p a n -> p (a n)") for t in (x3_hi, x3_lo))
                dve.tensor_tensor(lo, x3T[:, b * P:(b + 1) * P], hi.bitcast(F32), ALU.subtract).then_inc(x3_ready, 1)

            def gates(c):
                wait_apart(dve, lg_copied, c + 1)
                for b in range(NB):
                    ins = dve.max(top[:, b, :], lg[:, b, :])
                ins.then_inc(top_done, 1)
                dve.wait_ge(top_done, c + 1)
                dve.tensor_tensor(ex[:, :, :], lg[:, :, :], top[:, :, 0:1].to_broadcast([P, NB, EXPERTS]),
                                  ALU.subtract).then_inc(ex_in_done, 1)
                for b in range(NB):
                    ins = dve.max_index(topi[:, b, :], top[:, b, :], lg[:, b, :])
                ins.then_inc(topi_done, 1)
                dve.wait_ge(topi_done, c + 1)
                dve.tensor_copy(topf[:, :, :], topi[:, :, :]).then_inc(topf_done, 1)
                dve.wait_ge(topf_done, c + 1)
                number = expert_no[:, :].unsqueeze(1).to_broadcast([P, NB, EXPERTS])
                dve.tensor_tensor(is1[:, :, :], number, topf[:, :, 0:1].to_broadcast([P, NB, EXPERTS]), ALU.is_equal)
                dve.tensor_tensor(is2[:, :, :], number, topf[:, :, 1:2].to_broadcast([P, NB, EXPERTS]),
                                  ALU.is_equal).then_inc(gate_step, 1)
                dve.wait_ge(gate_step, 5 * c + 1)
                dve.tensor_tensor(is1[:, :, :], is1[:, :, :], is2[:, :, :], ALU.add)
                dve.wait_ge(ex_done, c + 1)
                dve.tensor_reduce(gden[:, :], ex[:, :, :], AX_X, ALU.add).then_inc(gate_step, 1)
                dve.wait_ge(gate_step, 5 * c + 2)
                dve.reciprocal(grden[:, :], gden[:, :])
                dve.tensor_tensor(is1[:, :, :], is1[:, :, :], ex[:, :, :], ALU.mult).then_inc(gate_step, 1)
                dve.wait_ge(gate_step, 5 * c + 3)
                dve.tensor_tensor(gate[:, :, :], is1[:, :, :], grden[:, :].unsqueeze(2).to_broadcast([P, NB, EXPERTS]),
                                  ALU.mult).then_inc(gate_step, 1)
                dve.wait_ge(gate_step, 5 * c + 4)
                hi = gcol[:, :, 0:EXPERTS]
                wait(dve, gT_ps, c)
                dve.tensor_copy(hi.bitcast(F32R), gate[:, :, :]).then_inc(gate_step, 1)
                dve.wait_ge(gate_step, 5 * c + 5)
                dve.tensor_tensor(gcol[:, :, EXPERTS:2 * EXPERTS], gate[:, :, :], hi, ALU.subtract).then_inc(gcol_ready, 1)

            def body(c, experts):
                p = c - 1

                def step(n):
                    if experts:
                        expert_step(p, n)

                wait_apart(dve, x_in, 16 * (c + 1))
                norm(X, xn, 2 * c + 1, xn_ready)
                dve.wait_ge(cT_ps, c + 1)
                wait(dve, lg_ps, c)
                dve.tensor_copy(cT[:, :], pT1[:, :]).then_inc(cT_ready, 1)
                step(0)
                step(1)
                dve.wait_ge(vs_ps, c + 1)
                dve.tensor_copy(Vs[:, :, :].rearrange("p b n -> p (b n)"), pO[:, :]).then_inc(vs_ready, 1)

                def low(ps, bias, i):
                    dve.wait_ge(ps, c + 1)
                    dve.wait_ge(qkhi_ready, i)
                    dve.scalar_tensor_tensor(out=qk_lo[:, :], in0=pT0[:, :], scalar=cols[:, bias:bias + 1],
                                             in1=qk_hi[:, :].bitcast(F32), op0=ALU.add,
                                             op1=ALU.subtract).then_inc(qklo_ready, 1)

                low(k_ps, BK, 2 * c + 1)
                step(2)
                dve.wait_ge(vx_ps, c + 1)
                wait(dve, vpad_ready, NB * c)
                dve.tensor_tensor(V4[:, :, :], tiles(pT1), bv[:, :].unsqueeze(1).to_broadcast([P, NB, P]),
                                  ALU.add).then_inc(vx_ready, 1)
                step(3)
                dve.wait_ge(ss_ps, c + 1)
                dve.tensor_reduce(smx[:, :], tiles(pS), AX_X, ALU.max).then_inc(smax_done, 1)
                dve.wait_ge(smax_done, c + 1)
                dve.tensor_scalar(nmx[:, :], smx[:, :], -SCALE_S, None, ALU.mult).then_inc(nmx_ready, 1)
                step(4)

                def stack(dst, ps, done, g):
                    dve.wait_ge(ps, GROUPS * c + g + 1)
                    dve.tensor_copy(dst[:, g, :], pT1[:, :]).then_inc(done, 1)

                wait(dve, st_ps, UNITS * c)
                stack(Kst, kst_ps, kst_d, 1)
                step(5)
                stack(Kst, kst_ps, kst_d, 3)
                step(6)
                dve.wait_ge(p_ready, c + 1)
                dve.reciprocal(srden[:, :], sden[:, :]).then_inc(srden_done, 1)
                dve.wait_ge(srden_done, c + 1)
                dve.wait_ge(pvs_ps, c + 1)
                for b in range(NB):
                    ins = dve.scalar_tensor_tensor(out=X[:, b, :], in0=cols_of(pS, b), scalar=srden[:, b:b + 1],
                                                   in1=X[:, b, :], op0=ALU.mult, op1=ALU.add)
                ins.then_inc(x1_done, 1)
                step(7)
                wait_apart(dve, x1_done, c + 1)
                norm(X, xn, 2 * c + 2, xn_ready)
                step(8)
                step(9)
                low(q_ps, BQ, 2 * c + 2)
                step(10)
                stack(Qst, qst_ps, qst_d, 1)
                step(11)
                stack(Qst, qst_ps, qst_d, 3)
                step(12)

                def unit_max(t):
                    b, g = divmod(t, GROUPS)
                    dve.wait_ge(s_ps, UNITS * c + t + 1)
                    dve.tensor_reduce(mx[:, b % 2, GROUPS * g:GROUPS * g + HPG], tiles(pS), AX_X,
                                      ALU.max).then_inc(max_done, 1)
                    if g == GROUPS - 1:
                        dve.wait_ge(max_done, UNITS * c + t + 1)
                        wait(dve, mT_ps, NB * c + b)
                        dve.tensor_scalar(mcol[:, 0:HEADS], mx[:, b % 2, :], -1.0, None, ALU.mult).then_inc(m_hi, 1)
                        dve.wait_ge(m_hi, NB * c + b + 1)
                        dve.scalar_tensor_tensor(out=mcol[:, HEADS:2 * HEADS], in0=mx[:, b % 2, :], scalar=-1.0,
                                                 in1=mcol[:, 0:HEADS], op0=ALU.mult,
                                                 op1=ALU.subtract).then_inc(mcol_ready, 1)

                def normalise(b):
                    i = NB * c + b + 1
                    wait_apart(dve, o_evac, i)
                    dve.stream_shuffle(Dsb[:, :, :].rearrange("p a n -> p (a n)"),
                                       Osb[:, :, :].rearrange("p a n -> p (a n)"),
                                       [16 * (k // 16) + 8 + k % 8 for k in range(32)]).then_inc(o_shuf, 1)
                    dve.wait_ge(o_shuf, i)
                    dve.reciprocal(Dsb[:, :, :], Dsb[:, :, :]).then_inc(o_rec, 1)
                    dve.wait_ge(o_rec, i)
                    wait(dve, wo_ps, i - 1)
                    dve.tensor_tensor(ON[:, :, :], Osb[:, :, :], Dsb[:, :, :], ALU.mult).then_inc(on_ready, 1)

                for t in range(AHEAD):
                    unit_max(t)
                step(13)
                for u in range(UNITS):
                    b, g = divmod(u, GROUPS)
                    if u + AHEAD < UNITS:
                        unit_max(u + AHEAD)
                    if g == 0 and b >= 2:
                        third_T(c, b - 2)
                    if g == 1 and b >= 1:
                        normalise(b - 1)
                    if g == 2 and b >= 1:
                        third_x2(c, b - 1)
                    if g == 3 and b >= 1:
                        third_norm(c, b - 1)
                    step(A_STEPS + u)
                third_T(c, NB - 2)
                normalise(NB - 1)
                step(30)
                third_x2(c, NB - 1)
                step(31)
                third_norm(c, NB - 1)
                step(34)
                third_T(c, NB - 1)
                dve.wait_ge(lg_ps, c + 1)
                dve.tensor_copy(lg[:, :, :].rearrange("p b e -> p (b e)"),
                                pG[:, 0:NB * EXPERTS]).then_inc(lg_copied, 1)
                if experts:
                    out_add(p)
                gates(c)

            body(0, False)
            body(1, True)
            with dve.Fori(2, CHUNKS) as c:
                body(c, True)
            for n in range(STEPS + 3):
                expert_step(CHUNKS - 1, n)
            out_add(CHUNKS - 1)

        @block.tensor
        def _(pe):
            last_G = [None, None]

            def take_G(reader, count):
                if last_G[0] is not None:
                    wait(pe, *last_G)
                last_G[0], last_G[1] = reader, count

            def up(p, n):
                e, k = divmod(n, KF)
                if n == 0:
                    pe.wait_ge(x3_ready, NB * (p + 1))
                wait(pe, relu_done, before(p, n, 2))
                rh, rl = (t[:, bass.ds(p % 2, 1), :].rearrange("p a n -> p (a n)") for t in (x3_hi, x3_lo))
                wh, wl = w1_hi[:, e, k * P:(k + 1) * P], w1_lo[:, e, k * P:(k + 1) * P]
                pe.matmul(pH[n % 2][:, :], wh, rh, start=True, stop=False)
                pe.matmul(pH[n % 2][:, :], wh, rl, start=False, stop=False)
                pe.matmul(pH[n % 2][:, :], wl, rh, start=False, stop=True).then_inc(up_ps, 1)

            def down(p, n):
                e, k = divmod(n, KF)
                pe.wait_ge(lo_ready, STEPS * p + n + 1)
                if k == 0:
                    wait(pe, y_scaled, EXPERTS * p + e)
                rh, rl = h_hi[:, n % 3, :], h_lo[:, n % 3, :]
                wh, wl = w2_hi[:, e, k, :], w2_lo[:, e, k, :]
                pe.matmul(pY[:, :], wh, rh, start=(k == 0), stop=False)
                pe.matmul(pY[:, :], wl, rh, start=False, stop=False)
                pe.matmul(pY[:, :], wh, rl, start=False, stop=(k == KF - 1)).then_inc(dn_ps, 1)

            def expert_step(p, n):
                if n < STEPS:
                    up(p, n)
                if LAG <= n < STEPS + LAG:
                    down(p, n - LAG)
                if n % KF == 2 and n < STEPS:
                    e = n // KF
                    pe.wait_ge(gT_ready, p + 1)
                    take_G(gb_ready, EXPERTS * p + e + 1)
                    pe.matmul(pG[:, :], expert_rows[:, e:e + 1].to_broadcast([P, P]), gT[:, :],
                              start=True, stop=True).then_inc(gb_ps, 1)

            def transposes(bank, src, done):
                for b in range(NB):
                    mm = pe.transpose(cols_of(bank, b), src(b), identf[:, :])
                mm.then_inc(done, 1)

            def products(bank, lhsT, rhs, done):
                for b in range(NB):
                    mm = pe.matmul(cols_of(bank, b), lhsT(b), rhs(b), start=True, stop=True)
                mm.then_inc(done, 1)

            def gates_T(p):
                pe.wait_ge(gcol_ready, p + 1)
                take_G(gT_ready, p + 1)
                transposes(pG, lambda b: gcol[:, b, :], gT_ps)

            def out_T(p):
                pe.wait_ge(y_added, (EXPERTS - 1) * (p + 1))
                take_G(out_ready, p + 1)
                transposes(pG, lambda b: cols_of(yacc, b), oT_ps)

            def body(c, experts):
                p = c - 1

                def step(n):
                    if experts:
                        expert_step(p, n)

                pe.wait_ge(xn_ready, 2 * c + 1)
                wait(pe, exp_done, UNITS * c)
                transposes(pT0, lambda b: xn[:, b, :], xT_ps)
                pe.wait_ge(c_in, 16 * (c + 1))
                transposes(pT1, lambda b: C[:, b, :], cT_ps)
                step(0)
                pe.wait_ge(xnT_ready, 2 * c + 1)
                wait(pe, max_done, UNITS * c)
                pe.matmul(pS[:, :], Aqk[:, :], xnT[:, :], start=True, stop=True).then_inc(g_ps, 1)
                if experts:
                    gates_T(p)
                step(1)
                wait(pe, o_evac, NB * c)
                products(pO, lambda b: cols_of(xnT, b), lambda b: wvs[:, :], vs_ps)
                pe.wait_ge(cT_ready, c + 1)
                pe.matmul(pT0[:, :], wkx[:, :], cT[:, :], start=True, stop=True).then_inc(k_ps, 1)
                step(2)
                products(pT1, lambda b: cols_of(cT, b), lambda b: wvx[:, :], vx_ps)
                step(3)
                pe.wait_ge(gt_ready, c + 1)
                products(pS, lambda b: cols_of(xnT, b), lambda b: cols_of(GT, b), ss_ps)
                step(4)

                def stack(hi_sel, lo_sel, g, done):
                    bank = pT[g % 2]
                    pe.matmul(bank[:, :], hi_sel[:, g, :], qk_hi[:, :], start=True, stop=False)
                    pe.matmul(bank[:, :], lo_sel[:, g, :], qk_lo[:, :], start=False, stop=True).then_inc(done, 1)

                pe.wait_ge(qklo_ready, 2 * c + 1)
                stack(k_hi_sel, k_lo_sel, 0, kst_ps)
                pe.wait_ge(vx_ready, c + 1)
                stack(k_hi_sel, k_lo_sel, 1, kst_ps)
                step(5)
                pe.wait_ge(kst_a, 2 * c + 1)
                stack(k_hi_sel, k_lo_sel, 2, kst_ps)
                pe.wait_ge(kst_d, 2 * c + 1)
                stack(k_hi_sel, k_lo_sel, 3, kst_ps)
                step(6)
                pe.wait_ge(p_ready, c + 1)
                pe.wait_ge(vs_ready, c + 1)
                transposes(pO, lambda b: cols_of(Ps, b), pt_ps)
                pe.wait_ge(pts_ready, c + 1)
                products(pS, lambda b: PTs[:, b, :], lambda b: Vs[:, b, :], pvs_ps)
                step(7)
                step(8)
                step(9)
                pe.wait_ge(xn_ready, 2 * c + 2)
                transposes(pO, lambda b: xn[:, b, :], xT_ps)
                pe.wait_ge(xnT_ready, 2 * c + 2)
                pe.wait_ge(kst_a, 2 * c + 2)
                pe.matmul(pT0[:, :], wqx[:, :], xnT[:, :], start=True, stop=True).then_inc(q_ps, 1)
                step(10)
                pe.wait_ge(qklo_ready, 2 * c + 2)
                stack(q_hi_sel, q_lo_sel, 0, qst_ps)
                pe.wait_ge(kst_d, 2 * c + 2)
                stack(q_hi_sel, q_lo_sel, 1, qst_ps)
                step(11)
                pe.wait_ge(qst_a, 2 * c + 1)
                stack(q_hi_sel, q_lo_sel, 2, qst_ps)
                pe.wait_ge(qst_d, 2 * c + 1)
                stack(q_hi_sel, q_lo_sel, 3, qst_ps)
                step(12)

                def scores(t):
                    b, g = divmod(t, GROUPS)
                    if g == 0:
                        pe.wait_ge(kbd_in[b % 2], 16 * HPG * (2 * c + b // 2 + 1))
                    if t == 0:
                        pe.wait_ge(qst_a, 2 * c + 2)
                        pe.wait_ge(qst_d, 2 * c + 2)
                        pe.wait_ge(x1_done, c + 1)
                    wait(pe, max_done, UNITS * c + t)
                    pe.matmul(pS[:, :], Qst[:, g, b * P:(b + 1) * P],
                              Kbd[:, b % 2, g, :, :].rearrange("p h k -> p (h k)"), start=True, stop=False)
                    pe.matmul(tiles(pS), identb[:, :], maskb[:, :].unsqueeze(1).to_broadcast([P, HPG, P]),
                              start=False, stop=True).then_inc(s_ps, 1)

                def maxima_T(b):
                    pe.wait_ge(mcol_ready, NB * c + b + 1)
                    take_G(mT_ready, NB * c + b + 1)
                    pe.transpose(pG_b, mcol[:, :], identb[:, :]).then_inc(mT_ps, 1)

                def scores_T(u):
                    b, g = divmod(u, GROUPS)
                    if g == 0:
                        pe.wait_ge(mT_ready, NB * c + b + 1)
                        pe.wait_ge(qbd_in[b % 2], 16 * HPG * (2 * c + b // 2 + 1))
                    wait(pe, exp_done, UNITS * c + u - 1)
                    bank = pT[u % 2]
                    pe.matmul(bank[:, :], Kst[:, g, b * P:(b + 1) * P],
                              Qbd[:, b % 2, g, :, :].rearrange("p h q -> p (h q)"), start=True, stop=False)
                    for j in range(HPG):
                        h = HPG * g + j
                        mm = pe.matmul(bank[:, j * P:(j + 1) * P], head_rows[:, h:h + 1].to_broadcast([P, P]),
                                       mT[:, b % 2, :], start=False, stop=(j == HPG - 1))
                    mm.then_inc(st_ps, 1)

                def values(u):
                    b, g = divmod(u, GROUPS)
                    pe.wait_ge(keep_done, UNITS * c + u + 1)
                    if g == 0:
                        pe.wait_ge(vpad_ready, NB * c + b + 1)
                        wait(pe, o_evac, NB * c + b)
                    for j in range(HPG):
                        h = HPG * g + j
                        half = h // 8
                        mm = pe.matmul(pO[:, half * P:(half + 1) * P], Vpad[:, b % 2, h, :],
                                       PT[:, u % 2, j * P:(j + 1) * P], start=(h % 8 == 0), stop=(h % 8 == 7))
                    mm.then_inc(pv_ps, 1)

                def project(b):
                    pe.wait_ge(on_ready, NB * c + b + 1)
                    take_G(x2_done, NB * c + b + 1)
                    pe.matmul(pG[:, 0:P], ON[:, 0, :], wo[:, 0, :], start=True, stop=False)
                    pe.matmul(pG[:, 0:P], ON[:, 1, :], wo[:, 1, :], start=False, stop=True).then_inc(wo_ps, 1)

                def third_T(b):
                    pe.wait_ge(x3n_ready, NB * c + b + 1)
                    take_G(x3T_ready, NB * c + b + 1)
                    pe.transpose(pG[:, 0:P], x3n[:, :], identf[:, :]).then_inc(x3T_ps, 1)

                for t in range(AHEAD):
                    scores(t)
                step(13)
                maxima_T(0)
                for u in range(UNITS):
                    b, g = divmod(u, GROUPS)
                    if u + AHEAD < UNITS:
                        scores(u + AHEAD)
                    scores_T(u)
                    if u >= 1:
                        values(u - 1)
                    step(A_STEPS + u)
                    if g == 1 and b >= 1:
                        project(b - 1)
                    if g == 3 and b + 1 < NB:
                        maxima_T(b + 1)
                    if g == 3 and b >= 1:
                        third_T(b - 1)
                values(UNITS - 1)
                step(30)
                project(NB - 1)
                step(31)
                step(32)
                step(33)
                third_T(NB - 1)
                pe.wait_ge(x3T_ready, NB * (c + 1))
                take_G(lg_copied, c + 1)
                for b in range(NB):
                    mm = pe.matmul(pG[:, b * EXPERTS:(b + 1) * EXPERTS], cols_of(x3T, b), gw[:, :],
                                   start=True, stop=True)
                mm.then_inc(lg_ps, 1)
                if experts:
                    out_T(p)

            pe.wait_ge(selected, 1)
            pe.wait_ge(wts_in, 16 * 8)
            pe.wait_ge(rows_in, 16 * 5)
            for i in range(3):
                mm = pe.transpose(cols_of(pH0, i), h_full[:, 0, i * P:(i + 1) * P], identf[:, :])
            mm.then_inc(setup_T, 1)
            pe.wait_ge(setup_cp, 1)
            pe.matmul(pH1[:, 0:P], h_full[:, 1, P:2 * P], h_full[:, 1, 2 * P:3 * P], start=True,
                      stop=True).then_inc(aqk_ps, 1)
            pe.wait_ge(aqk_ready, 1)
            pe.wait_ge(cast_done, 1)
            pe.wait_ge(wo_in, 16 * HEADS)
            body(0, False)
            pe.wait_ge(w_lo, 2 * EXPERTS)
            body(1, True)
            with pe.Fori(2, CHUNKS) as c:
                last_G[0], last_G[1] = out_ready, c - 1
                body(c, True)
            last_G[0], last_G[1] = out_ready, CHUNKS - 1
            gates_T(CHUNKS - 1)
            for n in range(STEPS + LAG):
                expert_step(CHUNKS - 1, n)
            out_T(CHUNKS - 1)


_INS = ['x', 'ctx_1024', 'L0_attn_W_query', 'L0_attn_W_key', 'L0_attn_W_value', 'L0_xattn_w_q', 'L0_xattn_b_q',
        'L0_xattn_w_k', 'L0_xattn_b_k', 'L0_xattn_w_v', 'L0_xattn_b_v', 'L0_xattn_w_o', 'L0_xattn_b_o',
        'L0_ffn_gate_w', 'L0_ffn_w1', 'L0_ffn_b1', 'L0_ffn_w2', 'L0_ffn_b2']


def kernel(**inputs):
    import numpy as _np
    import concourse.bacc as _bacc
    from concourse import mybir as _mybir
    from concourse.bass_utils import run_bass_kernel_spmd as _run

    nc = _bacc.Bacc("TRN2", target_bir_lowering=False, num_devices=1)
    arrays, args = {}, []
    for name in _INS:
        a = _np.ascontiguousarray(inputs[name])
        arrays[f"in_{name}_dram"] = a
        args.append(nc.dram_tensor(f"in_{name}_dram", a.shape, _mybir.dt.from_np(a.dtype), kind="ExternalInput").ap())
    out = nc.dram_tensor("out_0_dram", inputs['x'].shape, _mybir.dt.float32, kind="ExternalOutput").ap()
    decoder_layer(nc, *args, out)
    r = _run(nc, [arrays], core_ids=[0])
    return r.results[0]["out_0_dram"]
```

```python
from contextlib import ExitStack

import concourse.bass as bass
from concourse import mybir

F32 = mybir.dt.float32
F32R = mybir.dt.float32r
BF16 = mybir.dt.bfloat16
U32 = mybir.dt.uint32
ALU = mybir.AluOpType
ACT = mybir.ActivationFunctionType
AX_X = mybir.AxisListType.X

P = 128
NB = 4
TOK = NB * P
HEADS = 16
DH = P // HEADS
GROUPS = 4
HPG = HEADS // GROUPS
UNITS = NB * GROUPS
EXPERTS = 8
KF = 4
STEPS = EXPERTS * KF
RING = 3
LAG = 2
AHEAD = 5
MASKED = -1e30
EPS = 1e-5
SECOND_BANK = (1, 3)
W_STEPS = tuple(range(5, 13)) + tuple(range(20, 28))
NORM_UNIT = 1
A_STEPS = 15


def wait(eng, sem, value):
    if not isinstance(value, int) or value > 0:
        eng.wait_ge(sem, value)


def before(p, n, ring):
    return STEPS * p + max(n - ring + 1, 0)


def decoder_layer(nc, x, ctx_in, Wq_s, Wk_s, Wv_s, w_q, b_q, w_k, b_k, w_v, b_v, w_o, b_o,
                  gate_w, w1, b1, w2, b2, out):
    B = x.shape[0]
    CHUNKS = B // NB
    SCALE_S = float(P) ** -0.5
    SCALE_X = float(DH) ** -0.5
    x_v = x.rearrange("(c b) p d -> c p b d", b=NB)
    ctx_v = ctx_in.rearrange("(c b) p d -> c p b d", b=NB)
    out_v = out.rearrange("(c b) p d -> c p b d", b=NB)

    with ExitStack() as stack:
        def sb(name, shape, dt=F32):
            return stack.enter_context(nc.sbuf_tensor(name, shape, dt))

        def sem(name):
            return stack.enter_context(nc.semaphore(name))

        identf = sb("identf", [P, P])
        identb = sb("identb", [P, P], BF16)
        maskb = sb("maskb", [P, P], BF16)
        head_rows = sb("head_rows", [P, HEADS], BF16)
        expert_rows = sb("expert_rows", [P, EXPERTS], F32R)
        q_hi_sel = sb("q_hi_sel", [P, GROUPS, P], F32R)
        q_lo_sel = sb("q_lo_sel", [P, GROUPS, P], F32R)
        k_hi_sel = sb("k_hi_sel", [P, GROUPS, P], F32R)
        k_lo_sel = sb("k_lo_sel", [P, GROUPS, P], F32R)
        minus_half = sb("minus_half", [P, NB])
        expert_no = sb("expert_no", [P, EXPERTS])
        Aqk = sb("Aqk", [P, P])
        wvs = sb("wvs", [P, P])
        wqx = sb("wqx", [P, P])
        wkx = sb("wkx", [P, P])
        wvx = sb("wvx", [P, P])
        wo = sb("wo", [P, P])
        gw = sb("gw", [P, EXPERTS])
        cols = sb("cols", [P, 64])
        bv = sb("bv", [P, P])
        bo = sb("bo", [P, P])
        w1_hi = sb("w1_hi", [P, EXPERTS, TOK], F32R)
        w1_lo = sb("w1_lo", [P, EXPERTS, TOK], F32R)
        w2_hi = sb("w2_hi", [P, EXPERTS, KF, P], F32R)
        w2_lo = sb("w2_lo", [P, EXPERTS, KF, P], F32R)
        B1, B2, GW, BQ, BK = 0, STEPS, STEPS + 8, STEPS + 16, STEPS + 17
        X = sb("X", [P, 2, NB, P])
        C = sb("C", [P, NB, P])
        xn = sb("xn", [P, NB, P])
        PTs = xn
        xnT = sb("xnT", [P, TOK])
        cT = sb("cT", [P, TOK])
        Vs = C
        PT = sb("PT", [P, 2, TOK])
        Ps, GT = PT[:, 0, :], PT[:, 1, :]
        V4 = sb("V4", [P, NB, P])
        x3T = V4[:, :, :].rearrange("p b n -> p (b n)")
        qk_hi = sb("qk_hi", [P, TOK], F32R)
        qk_lo = sb("qk_lo", [P, TOK], F32R)
        Kst = sb("Kst", [P, GROUPS, TOK], F32R)
        Qst = sb("Qst", [P, GROUPS, TOK], F32R)
        Kbd = sb("Kbd", [P, 2, GROUPS, HPG, P], F32R)
        Qbd = sb("Qbd", [P, 2, GROUPS, HPG, P], F32R)
        Vpad = sb("Vpad", [P, 2, HEADS, P])
        smx = sb("smx", [P, NB])
        nmx = sb("nmx", [P, NB])
        sden = sb("sden", [P, NB])
        srden = sb("srden", [P, NB])
        mx = sb("mx", [P, 2, HEADS])
        mcol = sb("mcol", [P, P], BF16)
        mT = sb("mT", [P, 2, P], BF16)
        rden = sb("rden", [P, HEADS])
        On = sb("On", [P, P])
        OT = sb("OT", [P, P])
        x3n = OT
        st1 = sb("st1", [P, NB, 6])
        mv1 = sb("mv1", [P, NB, 2])
        ve1 = sb("ve1", [P, NB])
        rs1 = sb("rs1", [P, NB])
        st3 = sb("st3", [P, 6])
        mv3 = sb("mv3", [P, 2])
        ve3 = sb("ve3", [P, 1])
        rs3 = sb("rs3", [P, 1])
        x3_hi = sb("x3_hi", [P, 2, TOK], F32R)
        x3_lo = sb("x3_lo", [P, 2, TOK], F32R)
        h_hi = sb("h_hi", [P, RING, TOK], F32R)
        h_lo = sb("h_lo", [P, RING, TOK], F32R)
        work = sb("work", [P, 7 + 2, TOK])
        h_full, Gb, yt, yacc = work[:, 0:RING, :], work[:, 3:5, :], work[:, 5, :], work[:, 6, :]
        x2 = work[:, 7:9, :].rearrange("p a (b d) -> p a b d", b=NB)
        w_stage = work[:, 0:EXPERTS, :]
        lg = sb("lg", [P, NB, EXPERTS])
        ex = sb("ex", [P, NB, EXPERTS])
        top = sb("top", [P, NB, 8])
        topi = sb("topi", [P, NB, 8], U32)
        topf = sb("topf", [P, NB, 8])
        is1 = sb("is1", [P, NB, EXPERTS])
        is2 = sb("is2", [P, NB, EXPERTS])
        gden = sb("gden", [P, NB])
        grden = sb("grden", [P, NB])
        gate = sb("gate", [P, NB, EXPERTS])
        gcol = sb("gcol", [P, P + (NB - 1) * 2 * EXPERTS])
        gT = sb("gT", [P, TOK], F32R)

        def pb(name):
            return stack.enter_context(nc.psum_tensor(name, [P, TOK], F32))

        pS, pT0, pT1, pO, pG, pH0, pH1, pY = (pb(n) for n in ("pS", "pT0", "pT1", "pO", "pG", "pH0", "pH1", "pY"))
        pT = (pT0, pT1)
        pH = (pH0, pH1)
        pG_b = pG[:, 0:P // 2].bitcast(BF16)

        zeroed, ident_ready, selected, bd_zeroed, rows_in, wts_in, w1_in, w2_in = (
            sem(n) for n in ("zeroed", "ident_ready", "selected", "bd_zeroed", "rows_in", "wts_in", "w1_in", "w2_in"))
        cast_done, setup_T, setup_cp, aqk_ps, aqk_ready, w_hi, w_lo, vpad_init, sel_step = (
            sem(n) for n in ("cast_done", "setup_T", "setup_cp", "aqk_ps", "aqk_ready", "w_hi", "w_lo", "vpad_init", "sel_step"))
        x_in, c_in, out_done = sem("x_in"), sem("c_in"), sem("out_done")
        kbd_in = (sem("kbd_in0"), sem("kbd_in1"))
        qbd_in = (sem("qbd_in0"), sem("qbd_in1"))
        (ln_stat, ln_agg, ln_ve, ln_rstd, xn_ready, xT_ps, cT_ps, g_ps, vs_ps, k_ps, vx_ps, ss_ps, st_kps,
         xnT_ready, cT_ready, gt_ready, vs_ready, khi_ready, klo_ready, vx_ready, smax_done, nmx_ready, p_ready,
         kst_a, kst_d, pt_ps, pts_ready, pvs_ps, srden_done, x1_done, x1b_ready, q_ps, qst_ps, qst_a, qst_d) = (
            sem(n) for n in (
                "ln_stat", "ln_agg", "ln_ve", "ln_rstd", "xn_ready", "xT_ps", "cT_ps", "g_ps", "vs_ps", "k_ps",
                "vx_ps", "ss_ps", "kst_ps", "xnT_ready", "cT_ready", "gt_ready", "vs_ready", "qkhi_ready",
                "qklo_ready", "vx_ready", "smax_done", "nmx_ready", "p_ready", "kst_a", "kst_d", "pt_ps",
                "pts_ready", "pvs_ps", "srden_done", "x1_done", "x1b_ready", "q_ps", "qst_ps", "qst_a", "qst_d"))
        kst_ps, qkhi_ready, qklo_ready = st_kps, khi_ready, klo_ready
        (s_ps, max_done, m_hi, mcol_ready, mT_ps, mT_ready, st_ps, exp_done, keep_done, vpad_ready, pv_ps,
         o_rec, on_ready, ot_ps, ot_ready, wo_ps, x2_done, st3_done, mv3_done, ve3_done, rs3_done, x3n_ready,
         x3T_ps, x3hi_ready, x3T_ready, x3_ready) = (
            sem(n) for n in (
                "s_ps", "max_done", "m_hi", "mcol_ready", "mT_ps", "mT_ready", "st_ps", "exp_done", "keep_done",
                "vpad_ready", "pv_ps", "o_rec", "on_ready", "ot_ps", "ot_ready", "wo_ps", "x2_done", "st3_done",
                "mv3_done", "ve3_done", "rs3_done", "x3n_ready", "x3T_ps", "x3hi_ready", "x3T_ready", "x3_ready"))
        (lg_ps, lg_copied, top_done, topi_done, ex_in_done, ex_done, topf_done, gate_step, gcol_ready, gT_ps,
         gT_ready, gb_ps, gb_ready, up_ps, relu_done, lo_ready, dn_ps, y_scaled, y_added, oT_ps, out_ready) = (
            sem(n) for n in (
                "lg_ps", "lg_copied", "top_done", "topi_done", "ex_in_done", "ex_done", "topf_done", "gate_step",
                "gcol_ready", "gT_ps", "gT_ready", "gb_ps", "gb_ready", "up_ps", "relu_done", "lo_ready", "dn_ps",
                "y_scaled", "y_added", "oT_ps", "out_ready"))

        block = stack.enter_context(nc.Block())

        def wait_apart(eng, sem, value):
            if not isinstance(value, int):
                value = eng.to_reg(value)
                eng.wait_ge(selected, 1)
            wait(eng, sem, value)

        def X_of(c):
            return X[:, bass.ds(c % 2, 1), :, :].rearrange("p a b d -> p (a b) d")

        def cols_of(t, b):
            return t[:, b * P:(b + 1) * P]

        def tiles(t):
            return t[:, :].rearrange("p (b n) -> p b n", b=NB)

        @block.sync
        def _(sp):
            sp.dma_start(X[:, 0, :, :], x_v[0]).then_inc(x_in, 16)
            wts = ((Gb[:, 0, 0:P], Wq_s), (Gb[:, 0, P:2 * P], Wk_s), (wvs[:, :], Wv_s), (wqx[:, :], w_q),
                   (wkx[:, :], w_k), (wvx[:, :], w_v), (wo[:, :], w_o), (bv[:, :], b_v.partition_broadcast(P)),
                   (bo[:, :], b_o.partition_broadcast(P)))
            for dst, src in wts:
                sp.dma_start(dst, src).then_inc(wts_in, 16)
            sp.wait_ge(zeroed, 1)
            small = Gb[:, 0, 2 * P:3 * P]
            rows = ((B1, b1.rearrange("e (k p) -> (e k) p", p=P)), (B2, b2), (GW, gate_w),
                    (BQ, b_q.rearrange("(a n) -> a n", a=1)), (BK, b_k.rearrange("(a n) -> a n", a=1)))
            for r, src in rows:
                sp.dma_start(small[r:r + src.shape[0], :], src).then_inc(rows_in, 16)
            sp.dma_start(C[:, :, :], ctx_v[0]).then_inc(c_in, 16)
            sp.wait_ge(cast_done, 1)
            sp.wait_ge(aqk_ps, 1)
            sp.dma_start(w_stage, w1.rearrange("e h f -> h e f")).then_inc(w1_in, 16)

            def spread(bd, st, slot, b, done):
                for j in range(HPG):
                    sp.dma_start(bd[32 * j:32 * j + 32, slot, :, j, :].bitcast(F32),
                                 st[32 * j:32 * j + 32, :, b * P:(b + 1) * P].bitcast(F32)).then_inc(done[slot], 16)

            def transfers(c, last, experts):
                if not last:
                    wait_apart(sp, x2_done, NB * c)
                    sp.dma_start(X_of(c + 1), x_v[bass.ds(c + 1, 1)].rearrange("a p b d -> p (a b) d")).then_inc(x_in, 16)
                if not experts:
                    sp.wait_ge(bd_zeroed, 2)
                wait_apart(sp, kst_a, 2 * c + 2)
                wait_apart(sp, kst_d, 2 * c + 2)
                wait_apart(sp, s_ps, UNITS * c)
                spread(Kbd, Kst, 0, 0, kbd_in)
                spread(Kbd, Kst, 1, 1, kbd_in)
                wait_apart(sp, pvs_ps, c + 1)
                if not last:
                    sp.dma_start(C[:, :, :], ctx_v[bass.ds(c + 1, 1)].rearrange("a p b d -> p (a b) d")).then_inc(c_in, 16)
                wait_apart(sp, qst_a, 2 * c + 2)
                wait_apart(sp, qst_d, 2 * c + 2)
                wait_apart(sp, st_ps, UNITS * c)
                spread(Qbd, Qst, 0, 0, qbd_in)
                spread(Qbd, Qst, 1, 1, qbd_in)
                if not experts:
                    sp.wait_ge(w_lo, EXPERTS)
                    sp.dma_start(w_stage.rearrange("p e (k n) -> p e k n", k=KF),
                                 w2.rearrange("e (k p) h -> p e k h", p=P)).then_inc(w2_in, 16)
                wait_apart(sp, s_ps, UNITS * c + 4)
                spread(Kbd, Kst, 0, 2, kbd_in)
                wait_apart(sp, s_ps, UNITS * c + 8)
                spread(Kbd, Kst, 1, 3, kbd_in)
                wait_apart(sp, st_ps, UNITS * c + 4)
                spread(Qbd, Qst, 0, 2, qbd_in)
                wait_apart(sp, st_ps, UNITS * c + 8)
                spread(Qbd, Qst, 1, 3, qbd_in)
                if experts:
                    store(c - 1)

            def store(p):
                wait_apart(sp, out_ready, p + 1)
                src = x2[:, bass.ds((p + 1) % 2, 1), :, :].rearrange("p a b d -> p (a b) d")
                sp.dma_start(out_v[bass.ds(p, 1)].rearrange("a p b d -> p (a b) d"), src).then_inc(out_done, 16)

            transfers(0, False, False)
            transfers(1, False, True)
            with sp.Fori(2, CHUNKS - 1) as c:
                transfers(c, False, True)
            transfers(CHUNKS - 1, True, True)
            store(CHUNKS - 1)
            sp.wait_ge(out_done, 16 * CHUNKS)

        @block.gpsimd
        def _(pool):
            pool.memset(Gb[:, 0, 2 * P:3 * P], 0.0).then_inc(zeroed, 1)
            pool.memset(identf[:, :], 0.0).then_inc(sel_step, 1)
            pool.wait_ge(sel_step, 1)
            pool.affine_select(out=identf[:, :], in_=identf[:, :], compare_op=ALU.not_equal, fill=1.0, base=0,
                               pattern=[[-1, P]], channel_multiplier=1).then_inc(ident_ready, 1)
            pool.memset(maskb[:, :], 0.0)
            pool.memset(head_rows[:, :], 0.0)
            pool.memset(Gb[:, 1, 0:EXPERTS], 0.0)
            pool.memset(PT[:, :, :], 0.0)
            pool.memset(yacc[:, :], 0.0)
            pool.memset(V4[:, :, :], 0.0)
            pool.memset(minus_half[:, :], -0.5)
            for e in range(EXPERTS):
                pool.memset(expert_no[:, e:e + 1], float(e))
            pool.memset(gcol[:, :], 0.0)
            pool.memset(mcol[:, :], 0.0).then_inc(sel_step, 1)
            pool.wait_ge(sel_step, 2)
            pool.affine_select(out=maskb[:, :], in_=maskb[:, :], compare_op=ALU.is_ge, fill=MASKED, base=0,
                               pattern=[[-1, P]], channel_multiplier=1)
            pick = ((PT[:, 0, :], slice(0, 2)), (PT[:, 1, :], slice(2, 4)),
                    (yacc[:, :], slice(0, 4, 2)),
                    (V4[:, :, :].rearrange("p b n -> p (b n)"), slice(1, 4, 2)))
            for t, copies in pick:
                v = t.rearrange("p (h i d) -> p h i d", h=HEADS, d=DH)[:, :, copies, :]
                pool.affine_select(out=v, in_=v, compare_op=ALU.not_equal, fill=1.0, base=0,
                                   pattern=[[-DH, HEADS], [0, 2], [-1, DH]], channel_multiplier=1)
            for base in (0, -HEADS):
                pool.affine_select(out=head_rows[:, :], in_=head_rows[:, :], compare_op=ALU.not_equal, fill=1.0,
                                   base=base, pattern=[[-1, HEADS]], channel_multiplier=1).then_inc(sel_step, 1)
                pool.wait_ge(sel_step, 3 if base == 0 else 4)
            for base in (0, -EXPERTS):
                v = Gb[:, 1, 0:EXPERTS]
                pool.affine_select(out=v, in_=v, compare_op=ALU.not_equal, fill=1.0, base=base,
                                   pattern=[[-1, EXPERTS]], channel_multiplier=1).then_inc(sel_step, 1)
                if base == 0:
                    pool.wait_ge(sel_step, 5)
            pool.wait_ge(sel_step, 6)
            pool.memset(smx[:, :], 0.0).then_inc(selected, 1)

            def power(ve, rs, n):
                return pool.tensor_tensor(rs, ve, minus_half[:, 0:n], ALU.pow)

            def fill_vpad(c, b):
                wait_apart(pool, pv_ps, UNITS * c + GROUPS * (b - 1))
                wait_apart(pool, vx_ready, c + 1)
                w = P + 2 * DH
                for half in range(2):
                    flat = Vpad[:, b % 2, 8 * half:8 * half + 8, :].rearrange("p h n -> p (h n)")
                    vals = V4[:, b, 64 * half:64 * half + 64].rearrange("p (h d) -> p h d", d=DH)
                    pool.tensor_copy(flat[:, 0:7 * w].rearrange("p (h n) -> p h n", n=w)[:, :, 0:DH], vals[:, 0:7, :])
                    ins = pool.tensor_copy(flat[:, 7 * w:7 * w + DH], vals[:, 7, :])
                ins.then_inc(vpad_ready, 1)

            def keep_causal(c, u):
                wait_apart(pool, exp_done, UNITS * c + u + 1)
                v = PT[:, u % 2, :].rearrange("p (h q) -> p h q", h=HPG)
                pool.affine_select(out=v, in_=v, compare_op=ALU.is_ge, fill=0.0, base=0,
                                   pattern=[[0, HPG], [1, P]], channel_multiplier=-1).then_inc(keep_done, 1)

            def expert_step(p, n):
                e, r = divmod(n - 6, KF)
                if r == 0 and 1 <= e < EXPERTS:
                    pool.wait_ge(y_scaled, EXPERTS * p + e + 1)
                    pool.tensor_tensor(yacc[:, :], yacc[:, :], yt[:, :], ALU.add).then_inc(y_added, 1)
                    pool.wait_ge(y_added, (EXPERTS - 1) * p + e)

            def third_power(c, b):
                pool.wait_ge(ve3_done, NB * c + b + 1)
                power(ve3[:, :], rs3[:, :], 1).then_inc(rs3_done, 1)

            def norm_power(i):
                pool.wait_ge(ln_ve, i)
                power(ve1[:, :], rs1[:, :], NB).then_inc(ln_rstd, 1)

            def body(c, last, experts):
                p = c - 1

                def step(n):
                    if experts:
                        expert_step(p, n)

                for n in range(7):
                    step(n)
                norm_power(2 * c + 2)
                if not experts:
                    pool.wait_ge(vpad_init, 2)
                fill_vpad(c, 0)
                fill_vpad(c, 1)
                pool.wait_ge(xn_ready, 2 * c + 2)
                for b in range(NB):
                    ins = pool.tensor_tensor(X_of(c)[:, b, :], X_of(c)[:, b, :], bo[:, :], ALU.add)
                ins.then_inc(x1b_ready, 1)
                for n in range(7, A_STEPS):
                    step(n)
                for u in range(UNITS):
                    b, g = divmod(u, GROUPS)
                    keep_causal(c, u)
                    if g == 1 and 2 <= b + 1 < NB:
                        fill_vpad(c, b + 1)
                    if g == 2 and b >= 1:
                        third_power(c, b - 1)
                    if u == NORM_UNIT + 1 and not last:
                        norm_power(2 * c + 3)
                    step(A_STEPS + u)
                step(31)
                step(32)
                third_power(c, NB - 1)
                step(33)
                step(34)

            norm_power(1)
            pool.memset(Qbd[:, :, :, :, :].bitcast(F32), 0.0).then_inc(bd_zeroed, 1)
            body(0, False, False)
            body(1, False, True)
            with pool.Fori(2, CHUNKS - 1) as c:
                body(c, False, True)
            body(CHUNKS - 1, True, True)
            for n in range(STEPS + 3):
                expert_step(CHUNKS - 1, n)

        @block.scalar
        def _(act):
            def copy(dst, src):
                return act.activation(dst, src, ACT.Copy)

            def expert_step(p, n):
                if n < STEPS:
                    act.wait_ge(up_ps, STEPS * p + n + 1)
                    wait(act, dn_ps, before(p, n, RING))
                    act.activation(h_hi[:, n % RING, :], pH[n % 2][:, :], ACT.Relu, bias=cols[:, B1 + n:B1 + n + 1])
                    wait(act, lo_ready, before(p, n, RING))
                    act.activation(h_full[:, n % RING, :], pH[n % 2][:, :], ACT.Relu,
                                   bias=cols[:, B1 + n:B1 + n + 1]).then_inc(relu_done, 1)
                if n % KF == 3 and n < STEPS:
                    e = n // KF
                    act.wait_ge(gb_ps, EXPERTS * p + e + 1)
                    wait(act, y_scaled, EXPERTS * p + max(e - 1, 0))
                    copy(Gb[:, e % 2, :], pG[:, :]).then_inc(gb_ready, 1)

            def gates_T(p):
                act.wait_ge(gT_ps, p + 1)
                wait(act, gb_ps, EXPERTS * p)
                copy(gT[:, :], pG[:, :]).then_inc(gT_ready, 1)

            def stack_evac(dst, ps, done, c):
                for g in (0, 2):
                    act.wait_ge(ps, GROUPS * c + g + 1)
                    copy(dst[:, g, :], pT0[:, :]).then_inc(done, 1)
                    yield

            def third_T(c, b):
                act.wait_ge(x3T_ps, NB * c + b + 1)
                wait(act, oT_ps, c - 1)
                copy(x3_hi[:, bass.ds(c % 2, 1), b * P:(b + 1) * P].rearrange("p a n -> p (a n)"),
                     pG[:, 0:P]).then_inc(x3hi_ready, 1)

            def first_T(c):
                act.wait_ge(xT_ps, 2 * c + 1)
                copy(xnT[:, :], pT0[:, :]).then_inc(xnT_ready, 1)

            def gates_exp(p):
                act.wait_ge(ex_in_done, p + 1)
                act.activation(ex[:, :, :], ex[:, :, :], ACT.Exp).then_inc(ex_done, 1)

            def weights_hi(n):
                e = n % EXPERTS
                act.wait_ge(w1_in if n < EXPERTS else w2_in, 16)
                dst = w1_hi[:, e] if n < EXPERTS else w2_hi[:, e].rearrange("p k n -> p (k n)")
                copy(dst, w_stage[:, e, :]).then_inc(w_hi, 1)

            def body(c, last, experts):
                p = c - 1

                def step(n):
                    if experts:
                        expert_step(p, n)
                    elif n in W_STEPS:
                        weights_hi(W_STEPS.index(n))

                act.wait_ge(g_ps, c + 1)
                copy(GT, pS[:, :]).then_inc(gt_ready, 1)
                act.wait_ge(k_ps, c + 1)
                wait(act, qst_ps, GROUPS * c)
                act.activation(qk_hi[:, :], pT0[:, :], ACT.Identity, bias=cols[:, BK:BK + 1]).then_inc(qkhi_ready, 1)
                for b in range(NB):
                    act.wait_ge(nmx_ready, c + 1)
                    ins = act.activation(cols_of(Ps, b), cols_of(pS, b), ACT.Exp, bias=nmx[:, b:b + 1],
                                         scale=SCALE_S, accum_out=sden[:, b:b + 1])
                ins.then_inc(p_ready, 1)
                step(0)
                kst = stack_evac(Kst, kst_ps, kst_a, c)
                wait(act, st_ps, UNITS * c)
                next(kst)
                if experts:
                    gates_exp(p)
                step(1)
                next(kst)
                step(2)
                act.wait_ge(pt_ps, c + 1)
                copy(PTs[:, :, :].rearrange("p b n -> p (b n)"), pO[:, :]).then_inc(pts_ready, 1)
                if experts:
                    gates_T(p)
                for n in range(3, 9):
                    step(n)
                act.wait_ge(xT_ps, 2 * c + 2)
                copy(xnT[:, :], pO[:, :]).then_inc(xnT_ready, 1)
                step(9)
                act.wait_ge(q_ps, c + 1)
                act.wait_ge(kst_ps, GROUPS * (c + 1))
                act.activation(qk_hi[:, :], pT0[:, :], ACT.Identity, bias=cols[:, BQ:BQ + 1]).then_inc(qkhi_ready, 1)
                step(10)
                qst = stack_evac(Qst, qst_ps, qst_a, c)
                wait(act, s_ps, UNITS * c)
                next(qst)
                step(11)
                next(qst)
                step(12)
                step(13)
                step(14)

                def m_T(b):
                    act.wait_ge(mT_ps, NB * c + b + 1)
                    wait(act, st_ps, UNITS * c + GROUPS * (b - 1))
                    copy(mT[:, b % 2, :], pG_b).then_inc(mT_ready, 1)

                def o_T(b):
                    act.wait_ge(ot_ps, NB * c + b + 1)
                    wait(act, x3T_ps, NB * c + b)
                    copy(OT[:, :], pG[:, 0:P]).then_inc(ot_ready, 1)

                m_T(0)
                for u in range(UNITS):
                    b, g = divmod(u, GROUPS)
                    act.wait_ge(st_ps, UNITS * c + u + 1)
                    wait(act, pv_ps, UNITS * c + u - 1)
                    act.activation(PT[:, u % 2, :], pT[u % 2][:, :], ACT.Exp, scale=SCALE_X).then_inc(exp_done, 1)
                    if g == 0 and b >= 2:
                        third_T(c, b - 2)
                    if g == 1 and b >= 1:
                        o_T(b - 1)
                    if g == 3 and b + 1 < NB:
                        m_T(b + 1)
                    step(A_STEPS + u)
                third_T(c, NB - 2)
                step(31)
                if not last:
                    first_T(c + 1)
                o_T(NB - 1)
                third_T(c, NB - 1)

            act.wait_ge(sel_step, 2)
            act.activation(srden[:, 0:1], minus_half[:, 0:1], ACT.Exp)
            first_T(0)
            act.wait_ge(cast_done, 1)
            body(0, False, False)
            body(1, False, True)
            with act.Fori(2, CHUNKS - 1) as c:
                body(c, False, True)
            body(CHUNKS - 1, True, True)
            gates_exp(CHUNKS - 1)
            gates_T(CHUNKS - 1)
            for n in range(STEPS):
                expert_step(CHUNKS - 1, n)

        @block.vector
        def _(dve):
            def norm_stats(src, i):
                for b in range(NB):
                    ins = dve.bn_stats(st1[:, b, :], src[:, b, :])
                ins.then_inc(ln_stat, 1)
                wait_apart(dve, ln_stat, i)
                for b in range(NB):
                    ins = dve.bn_aggr(mv1[:, b, :], st1[:, b, :])
                ins.then_inc(ln_agg, 1)
                dve.wait_ge(ln_agg, i)
                dve.tensor_scalar(ve1[:, :], mv1[:, :, 1], EPS, None, ALU.add).then_inc(ln_ve, 1)

            def norm_apply(src, i, batches=range(NB)):
                dve.wait_ge(ln_rstd, i)
                for b in batches:
                    ins = dve.tensor_scalar(xn[:, b, :], src[:, b, :], mv1[:, b, 0:1], rs1[:, b:b + 1],
                                            ALU.subtract, ALU.mult)
                if b == NB - 1:
                    ins.then_inc(xn_ready, 1)

            def vpad_constants():
                dve.memset(Vpad[:, :, :, :], 0.0).then_inc(vpad_init, 1)
                dve.wait_ge(vpad_init, 1)
                for s in range(2):
                    for h in range(HEADS):
                        c0 = 2 * DH * (h % 8) + DH
                        ins = dve.memset(Vpad[:, s, h, c0:c0 + DH], 1.0)
                ins.then_inc(vpad_init, 1)

            vpad_constants()
            dve.memset(Kbd[:, :, :, :, :].bitcast(F32), 0.0).then_inc(bd_zeroed, 1)
            dve.wait_ge(x_in, 16)
            norm_stats(X_of(0), 1)
            dve.wait_ge(selected, 1)
            dve.tensor_copy(identb[:, :], identf[:, :])
            for t, src in ((q_hi_sel, PT[:, 0, :]), (q_lo_sel, PT[:, 1, :]),
                           (k_hi_sel, yacc[:, :]),
                           (k_lo_sel, V4[:, :, :].rearrange("p b n -> p (b n)"))):
                dve.tensor_copy(t[:, :, :].rearrange("p g n -> p (g n)"), src)
            dve.tensor_copy(expert_rows[:, :], Gb[:, 1, 0:EXPERTS]).then_inc(cast_done, 1)

            dve.wait_ge(setup_T, 1)
            dve.tensor_copy(Gb[:, 1, P:3 * P], pH0[:, 0:2 * P])
            dve.tensor_copy(cols[:, :], pH0[:, 2 * P:2 * P + 64])
            dve.tensor_copy(gw[:, :], pH0[:, 2 * P + GW:2 * P + GW + EXPERTS]).then_inc(setup_cp, 1)
            norm_apply(X_of(0), 1)
            dve.wait_ge(aqk_ps, 1)
            dve.tensor_copy(Aqk[:, :], pH1[:, 0:P]).then_inc(aqk_ready, 1)

            def weights_lo(n):
                e = n % EXPERTS
                hi, lo = (w1_hi[:, e], w1_lo[:, e]) if n < EXPERTS else (
                    t[:, e].rearrange("p k n -> p (k n)") for t in (w2_hi, w2_lo))
                dve.wait_ge(w_hi, n + 1)
                dve.tensor_tensor(lo, w_stage[:, e, :], hi.bitcast(F32), ALU.subtract).then_inc(w_lo, 1)

            def expert_scale(p, e):
                dve.wait_ge(dn_ps, STEPS * p + KF * (e + 1))
                dve.wait_ge(gb_ready, EXPERTS * p + e + 1)
                if e == 0:
                    wait(dve, oT_ps, p)
                else:
                    wait(dve, y_added, (EXPERTS - 1) * p + e - 1)
                dve.scalar_tensor_tensor(out=(yacc if e == 0 else yt)[:, :], in0=pY[:, :],
                                         scalar=cols[:, B2 + e:B2 + e + 1], in1=Gb[:, e % 2, :],
                                         op0=ALU.add, op1=ALU.mult).then_inc(y_scaled, 1)

            def expert_step(p, n):
                e, r = divmod(n - LAG - KF + 1, KF)
                if r == 0 and e >= 0:
                    expert_scale(p, e)
                if n < STEPS:
                    dve.wait_ge(relu_done, STEPS * p + n + 1)
                    wait(dve, dn_ps, before(p, n, RING))
                    dve.tensor_tensor(h_lo[:, n % RING, :], h_full[:, n % RING, :], h_hi[:, n % RING, :].bitcast(F32),
                                      ALU.subtract).then_inc(lo_ready, 1)

            def out_add(p):
                dve.wait_ge(oT_ps, p + 1)
                v = x2[:, bass.ds((p + 1) % 2, 1), :, :].rearrange("p a b d -> p (a b d)")
                dve.tensor_tensor(v, pG[:, :], v, ALU.add).then_inc(out_ready, 1)

            def third_x2(c, b):
                v = x2[:, bass.ds((c + 1) % 2, 1), b, :].rearrange("p a d -> p (a d)")
                dve.wait_ge(wo_ps, NB * c + b + 1)
                dve.wait_ge(x1b_ready, c + 1)
                if b == 0:
                    wait(dve, out_done, 16 * (c - 1))
                dve.tensor_tensor(v, pG[:, 0:P], X_of(c)[:, b, :], ALU.add).then_inc(x2_done, 1)
                wait_apart(dve, x2_done, NB * c + b + 1)
                dve.bn_stats(st3[:, :], v).then_inc(st3_done, 1)
                wait_apart(dve, st3_done, NB * c + b + 1)
                dve.bn_aggr(mv3[:, :], st3[:, :]).then_inc(mv3_done, 1)
                dve.wait_ge(mv3_done, NB * c + b + 1)
                dve.tensor_scalar(ve3[:, :], mv3[:, 1:2], EPS, None, ALU.add).then_inc(ve3_done, 1)

            def third_norm(c, b):
                dve.wait_ge(rs3_done, NB * c + b + 1)
                wait(dve, x3T_ps, NB * c + b)
                v = x2[:, bass.ds((c + 1) % 2, 1), b, :].rearrange("p a d -> p (a d)")
                dve.tensor_scalar(x3n[:, :], v, mv3[:, 0:1], rs3[:, :], ALU.subtract, ALU.mult).then_inc(x3n_ready, 1)

            def third_T(c, b):
                dve.wait_ge(x3T_ps, NB * c + b + 1)
                dve.wait_ge(x3hi_ready, NB * c + b + 1)
                dve.wait_ge(vpad_ready, NB * c + b + 1)
                dve.tensor_copy(x3T[:, b * P:(b + 1) * P], pG[:, 0:P]).then_inc(x3T_ready, 1)
                dve.wait_ge(x3T_ready, NB * c + b + 1)
                hi, lo = (t[:, bass.ds(c % 2, 1), b * P:(b + 1) * P].rearrange("p a n -> p (a n)") for t in (x3_hi, x3_lo))
                dve.tensor_tensor(lo, x3T[:, b * P:(b + 1) * P], hi.bitcast(F32), ALU.subtract).then_inc(x3_ready, 1)

            def gates_softmax(c):
                wait_apart(dve, lg_copied, c + 1)
                for b in range(NB):
                    ins = dve.max(top[:, b, :], lg[:, b, :])
                ins.then_inc(top_done, 1)
                dve.wait_ge(top_done, c + 1)
                dve.tensor_tensor(ex[:, :, :], lg[:, :, :], top[:, :, 0:1].to_broadcast([P, NB, EXPERTS]),
                                  ALU.subtract).then_inc(ex_in_done, 1)

            def gates_top(c):
                for b in range(NB):
                    ins = dve.max_index(topi[:, b, :], top[:, b, :], lg[:, b, :])
                ins.then_inc(topi_done, 1)
                dve.wait_ge(topi_done, c + 1)
                dve.tensor_copy(topf[:, :, :], topi[:, :, :]).then_inc(topf_done, 1)
                dve.wait_ge(topf_done, c + 1)
                number = expert_no[:, :].unsqueeze(1).to_broadcast([P, NB, EXPERTS])
                dve.tensor_tensor(is1[:, :, :], number, topf[:, :, 0:1].to_broadcast([P, NB, EXPERTS]), ALU.is_equal)
                dve.tensor_tensor(is2[:, :, :], number, topf[:, :, 1:2].to_broadcast([P, NB, EXPERTS]),
                                  ALU.is_equal).then_inc(gate_step, 1)
                dve.wait_ge(gate_step, 5 * c + 1)
                dve.tensor_tensor(is1[:, :, :], is1[:, :, :], is2[:, :, :], ALU.add)
                dve.wait_ge(ex_done, c + 1)
                dve.tensor_reduce(gden[:, :], ex[:, :, :], AX_X, ALU.add).then_inc(gate_step, 1)
                dve.wait_ge(gate_step, 5 * c + 2)
                dve.reciprocal(grden[:, :], gden[:, :])
                dve.tensor_tensor(is1[:, :, :], is1[:, :, :], ex[:, :, :], ALU.mult).then_inc(gate_step, 1)
                dve.wait_ge(gate_step, 5 * c + 3)
                dve.tensor_tensor(gate[:, :, :], is1[:, :, :], grden[:, :].unsqueeze(2).to_broadcast([P, NB, EXPERTS]),
                                  ALU.mult).then_inc(gate_step, 1)
                dve.wait_ge(gate_step, 5 * c + 4)
                both = gcol[:, 0:2 * EXPERTS * NB].rearrange("p (b n) -> p b n", b=NB)
                hi = both[:, :, 0:EXPERTS]
                wait(dve, gT_ps, c)
                dve.tensor_copy(hi.bitcast(F32R), gate[:, :, :]).then_inc(gate_step, 1)
                dve.wait_ge(gate_step, 5 * c + 5)
                dve.tensor_tensor(both[:, :, EXPERTS:2 * EXPERTS], gate[:, :, :], hi, ALU.subtract).then_inc(gcol_ready, 1)

            def body(c, last, experts):
                p = c - 1

                def step(n):
                    if experts:
                        expert_step(p, n)
                    elif n in W_STEPS:
                        weights_lo(W_STEPS.index(n))

                dve.wait_ge(cT_ps, c + 1)
                dve.tensor_copy(cT[:, :], pT1[:, :]).then_inc(cT_ready, 1)
                dve.wait_ge(vs_ps, c + 1)
                dve.tensor_copy(Vs[:, :, :].rearrange("p b n -> p (b n)"), pO[:, :]).then_inc(vs_ready, 1)

                def low(ps, bias, i):
                    dve.wait_ge(ps, c + 1)
                    dve.wait_ge(qkhi_ready, i)
                    dve.scalar_tensor_tensor(out=qk_lo[:, :], in0=pT0[:, :], scalar=cols[:, bias:bias + 1],
                                             in1=qk_hi[:, :].bitcast(F32), op0=ALU.add,
                                             op1=ALU.subtract).then_inc(qklo_ready, 1)

                low(k_ps, BK, 2 * c + 1)
                dve.wait_ge(ss_ps, c + 1)
                dve.tensor_reduce(smx[:, :], tiles(pS), AX_X, ALU.max).then_inc(smax_done, 1)
                dve.wait_ge(smax_done, c + 1)
                dve.tensor_scalar(nmx[:, :], smx[:, :], -SCALE_S, None, ALU.mult).then_inc(nmx_ready, 1)
                dve.wait_ge(vx_ps, c + 1)
                wait(dve, lg_ps, c)
                wait(dve, x3_ready, NB * c)
                dve.tensor_tensor(V4[:, :, :], tiles(pT1), bv[:, :].unsqueeze(1).to_broadcast([P, NB, P]),
                                  ALU.add).then_inc(vx_ready, 1)
                if experts:
                    gates_softmax(p)

                def stack(dst, ps, done, g):
                    dve.wait_ge(ps, GROUPS * c + g + 1)
                    dve.tensor_copy(dst[:, g, :], pT1[:, :]).then_inc(done, 1)

                wait(dve, st_ps, UNITS * c)
                step(0)
                stack(Kst, kst_ps, kst_d, 1)
                if experts:
                    gates_top(p)
                step(1)
                stack(Kst, kst_ps, kst_d, 3)
                dve.wait_ge(p_ready, c + 1)
                dve.reciprocal(srden[:, :], sden[:, :]).then_inc(srden_done, 1)
                step(2)
                step(3)
                dve.wait_ge(srden_done, c + 1)
                dve.wait_ge(pvs_ps, c + 1)
                for b in range(NB):
                    ins = dve.scalar_tensor_tensor(out=X_of(c)[:, b, :], in0=cols_of(pS, b), scalar=srden[:, b:b + 1],
                                                   in1=X_of(c)[:, b, :], op0=ALU.mult, op1=ALU.add)
                ins.then_inc(x1_done, 1)
                step(4)
                wait_apart(dve, x1_done, c + 1)
                norm_stats(X_of(c), 2 * c + 2)
                step(5)
                step(6)
                norm_apply(X_of(c), 2 * c + 2)
                step(7)
                step(8)
                step(9)
                low(q_ps, BQ, 2 * c + 2)
                step(10)
                stack(Qst, qst_ps, qst_d, 1)
                step(11)
                stack(Qst, qst_ps, qst_d, 3)

                def unit_max(t):
                    b, g = divmod(t, GROUPS)
                    dve.wait_ge(s_ps, UNITS * c + t + 1)
                    bank = pO if t in SECOND_BANK else pS
                    dve.tensor_reduce(mx[:, b % 2, GROUPS * g:GROUPS * g + HPG], tiles(bank), AX_X,
                                      ALU.max).then_inc(max_done, 1)
                    if g == GROUPS - 1:
                        dve.wait_ge(max_done, UNITS * c + t + 1)
                        wait(dve, mT_ps, NB * c + b)
                        dve.tensor_scalar(mcol[:, 0:HEADS], mx[:, b % 2, :], -1.0, None, ALU.mult).then_inc(m_hi, 1)
                        dve.wait_ge(m_hi, NB * c + b + 1)
                        dve.scalar_tensor_tensor(out=mcol[:, HEADS:2 * HEADS], in0=mx[:, b % 2, :], scalar=-1.0,
                                                 in1=mcol[:, 0:HEADS], op0=ALU.mult,
                                                 op1=ALU.subtract).then_inc(mcol_ready, 1)

                def normalise(b):
                    i = NB * c + b + 1
                    heads = pO[:, 0:2 * P].rearrange("p (h n) -> p h n", h=HEADS)
                    dve.wait_ge(pv_ps, UNITS * c + GROUPS * (b + 1))
                    dve.reciprocal(rden[:, :], heads[:, :, DH]).then_inc(o_rec, 1)
                    dve.wait_ge(o_rec, i)
                    wait(dve, ot_ps, i - 1)
                    dve.tensor_tensor(On[:, :].rearrange("p (h d) -> p h d", h=HEADS), heads[:, :, 0:DH],
                                      rden[:, :].unsqueeze(2).to_broadcast([P, HEADS, DH]),
                                      ALU.mult).then_inc(on_ready, 1)

                unit_max(0)
                step(12)
                unit_max(1)
                unit_max(2)
                step(13)
                unit_max(3)
                step(14)
                unit_max(4)
                for u in range(UNITS):
                    b, g = divmod(u, GROUPS)
                    if u + AHEAD < UNITS:
                        unit_max(u + AHEAD)
                    if g == 0 and b >= 2:
                        third_T(c, b - 2)
                    if g == 2 and b >= 1:
                        third_x2(c, b - 1)
                    if g == 3 and b >= 1:
                        third_norm(c, b - 1)
                    step(A_STEPS + u)
                    if g == 0 and b >= 1:
                        normalise(b - 1)
                    if u == NORM_UNIT and not last:
                        wait_apart(dve, x_in, 16 * (c + 2))
                        norm_stats(X_of(c + 1), 2 * c + 3)
                    if u == NORM_UNIT + 1 and not last:
                        norm_apply(X_of(c + 1), 2 * c + 3, range(2))
                    if u == NORM_UNIT + 2 and not last:
                        norm_apply(X_of(c + 1), 2 * c + 3, range(2, NB))
                third_T(c, NB - 2)
                normalise(NB - 1)
                step(31)
                third_x2(c, NB - 1)
                step(33)
                third_norm(c, NB - 1)
                third_T(c, NB - 1)
                if experts:
                    out_add(p)
                dve.wait_ge(lg_ps, c + 1)
                dve.tensor_copy(lg[:, :, :].rearrange("p b e -> p (b e)"),
                                pG[:, 0:NB * EXPERTS]).then_inc(lg_copied, 1)

            body(0, False, False)
            body(1, False, True)
            with dve.Fori(2, CHUNKS - 1) as c:
                body(c, False, True)
            body(CHUNKS - 1, True, True)
            gates_softmax(CHUNKS - 1)
            gates_top(CHUNKS - 1)
            for n in range(STEPS + 3):
                expert_step(CHUNKS - 1, n)
            out_add(CHUNKS - 1)

        @block.tensor
        def _(pe):
            last_G = [None, None]

            def take_G(reader, count):
                if last_G[0] is not None:
                    wait(pe, *last_G)
                last_G[0], last_G[1] = reader, count

            def up(p, n):
                e, k = divmod(n, KF)
                if n == 0:
                    pe.wait_ge(x3_ready, NB * (p + 1))
                wait(pe, relu_done, before(p, n, 2))
                rh, rl = (t[:, bass.ds(p % 2, 1), :].rearrange("p a n -> p (a n)") for t in (x3_hi, x3_lo))
                wh, wl = w1_hi[:, e, k * P:(k + 1) * P], w1_lo[:, e, k * P:(k + 1) * P]
                pe.matmul(pH[n % 2][:, :], wh, rh, start=True, stop=False)
                pe.matmul(pH[n % 2][:, :], wh, rl, start=False, stop=False)
                pe.matmul(pH[n % 2][:, :], wl, rh, start=False, stop=True).then_inc(up_ps, 1)

            def down(p, n):
                e, k = divmod(n, KF)
                pe.wait_ge(lo_ready, STEPS * p + n + 1)
                if k == 0:
                    wait(pe, y_scaled, EXPERTS * p + e)
                rh, rl = h_hi[:, n % RING, :], h_lo[:, n % RING, :]
                wh, wl = w2_hi[:, e, k, :], w2_lo[:, e, k, :]
                pe.matmul(pY[:, :], wh, rh, start=(k == 0), stop=False)
                pe.matmul(pY[:, :], wl, rh, start=False, stop=False)
                pe.matmul(pY[:, :], wh, rl, start=False, stop=(k == KF - 1)).then_inc(dn_ps, 1)

            def expert_step(p, n, between=None):
                if n < STEPS:
                    up(p, n)
                if between is not None:
                    between()
                if LAG <= n < STEPS + LAG:
                    down(p, n - LAG)
                if n % KF == 3 and n < STEPS:
                    e = n // KF
                    pe.wait_ge(gT_ready, p + 1)
                    take_G(gb_ready, EXPERTS * p + e + 1)
                    pe.matmul(pG[:, :], expert_rows[:, e:e + 1].to_broadcast([P, P]), gT[:, :],
                              start=True, stop=True).then_inc(gb_ps, 1)

            def transposes(bank, src, done):
                for b in range(NB):
                    mm = pe.transpose(cols_of(bank, b), src(b), identf[:, :])
                mm.then_inc(done, 1)

            def products(bank, lhsT, rhs, done):
                for b in range(NB):
                    mm = pe.matmul(cols_of(bank, b), lhsT(b), rhs(b), start=True, stop=True)
                mm.then_inc(done, 1)

            def gates_T(p):
                pe.wait_ge(gcol_ready, p + 1)
                take_G(gT_ready, p + 1)
                transposes(pG, lambda b: gcol[:, 2 * EXPERTS * b:2 * EXPERTS * b + P], gT_ps)

            def out_T(p):
                pe.wait_ge(y_added, (EXPERTS - 1) * (p + 1))
                take_G(out_ready, p + 1)
                transposes(pG, lambda b: cols_of(yacc, b), oT_ps)

            def first_T(c):
                pe.wait_ge(xn_ready, 2 * c + 1)
                wait(pe, exp_done, UNITS * c)
                transposes(pT0, lambda b: xn[:, b, :], xT_ps)

            def context_T(c):
                pe.wait_ge(c_in, 16 * (c + 1))
                transposes(pT1, lambda b: C[:, b, :], cT_ps)

            def self_queries(c):
                pe.wait_ge(xnT_ready, 2 * c + 1)
                wait(pe, max_done, UNITS * c)
                pe.matmul(pS[:, :], Aqk[:, :], xnT[:, :], start=True, stop=True).then_inc(g_ps, 1)

            def self_values(c):
                wait(pe, on_ready, NB * c)
                products(pO, lambda b: cols_of(xnT, b), lambda b: wvs[:, :], vs_ps)

            def body(c, last, experts):
                p = c - 1

                def step(n, between=None):
                    if experts:
                        expert_step(p, n, between)
                    elif between is not None:
                        between()

                pe.wait_ge(cT_ready, c + 1)
                pe.matmul(pT0[:, :], wkx[:, :], cT[:, :], start=True, stop=True).then_inc(k_ps, 1)
                pe.wait_ge(gt_ready, c + 1)
                products(pS, lambda b: cols_of(xnT, b), lambda b: cols_of(GT, b), ss_ps)
                products(pT1, lambda b: cols_of(cT, b), lambda b: wvx[:, :], vx_ps)
                step(0)

                def stack(hi_sel, lo_sel, g, done):
                    bank = pT[g % 2]
                    pe.matmul(bank[:, :], hi_sel[:, g, :], qk_hi[:, :], start=True, stop=False)
                    pe.matmul(bank[:, :], lo_sel[:, g, :], qk_lo[:, :], start=False, stop=True).then_inc(done, 1)

                pe.wait_ge(qklo_ready, 2 * c + 1)
                stack(k_hi_sel, k_lo_sel, 0, kst_ps)
                pe.wait_ge(vx_ready, c + 1)
                stack(k_hi_sel, k_lo_sel, 1, kst_ps)
                step(1)
                pe.wait_ge(kst_a, 2 * c + 1)
                stack(k_hi_sel, k_lo_sel, 2, kst_ps)
                pe.wait_ge(kst_d, 2 * c + 1)
                stack(k_hi_sel, k_lo_sel, 3, kst_ps)
                step(2)
                pe.wait_ge(p_ready, c + 1)
                pe.wait_ge(vs_ready, c + 1)
                transposes(pO, lambda b: cols_of(Ps, b), pt_ps)
                if experts:
                    gates_T(p)
                step(3)
                pe.wait_ge(pts_ready, c + 1)
                products(pS, lambda b: PTs[:, b, :], lambda b: Vs[:, b, :], pvs_ps)
                for n in range(4, 9):
                    step(n)
                pe.wait_ge(xn_ready, 2 * c + 2)
                transposes(pO, lambda b: xn[:, b, :], xT_ps)
                step(9)
                pe.wait_ge(xnT_ready, 2 * c + 2)
                pe.wait_ge(kst_a, 2 * c + 2)
                pe.matmul(pT0[:, :], wqx[:, :], xnT[:, :], start=True, stop=True).then_inc(q_ps, 1)
                step(10)
                pe.wait_ge(qklo_ready, 2 * c + 2)
                stack(q_hi_sel, q_lo_sel, 0, qst_ps)
                pe.wait_ge(kst_d, 2 * c + 2)
                stack(q_hi_sel, q_lo_sel, 1, qst_ps)
                step(11)
                pe.wait_ge(qst_a, 2 * c + 1)
                stack(q_hi_sel, q_lo_sel, 2, qst_ps)
                pe.wait_ge(qst_d, 2 * c + 1)
                stack(q_hi_sel, q_lo_sel, 3, qst_ps)

                def scores(t):
                    b, g = divmod(t, GROUPS)
                    if g == 0:
                        pe.wait_ge(kbd_in[b % 2], 16 * HPG * (2 * c + b // 2 + 1))
                    if t == 0:
                        pe.wait_ge(x1_done, c + 1)
                    if t < GROUPS:
                        pe.wait_ge((qst_a, qst_d)[g % 2], 2 * c + 1 + g // 2)
                    bank = pO if t in SECOND_BANK else pS
                    wait(pe, max_done, UNITS * c + (t if t >= AHEAD else max(t - 1, 0)))
                    pe.matmul(bank[:, :], Qst[:, g, b * P:(b + 1) * P],
                              Kbd[:, b % 2, g, :, :].rearrange("p h k -> p (h k)"), start=True, stop=False)
                    pe.matmul(tiles(bank), identb[:, :], maskb[:, :].unsqueeze(1).to_broadcast([P, HPG, P]),
                              start=False, stop=True).then_inc(s_ps, 1)

                def maxima_T(b):
                    pe.wait_ge(mcol_ready, NB * c + b + 1)
                    take_G(mT_ready, NB * c + b + 1)
                    pe.transpose(pG_b, mcol[:, :], identb[:, :]).then_inc(mT_ps, 1)

                def scores_T(u):
                    b, g = divmod(u, GROUPS)
                    if g == 0:
                        pe.wait_ge(mT_ready, NB * c + b + 1)
                        pe.wait_ge(qbd_in[b % 2], 16 * HPG * (2 * c + b // 2 + 1))
                    wait(pe, exp_done, UNITS * c + u - 1)
                    bank = pT[u % 2]
                    pe.matmul(bank[:, :], Kst[:, g, b * P:(b + 1) * P],
                              Qbd[:, b % 2, g, :, :].rearrange("p h q -> p (h q)"), start=True, stop=False)
                    for j in range(HPG):
                        h = HPG * g + j
                        mm = pe.matmul(bank[:, j * P:(j + 1) * P], head_rows[:, h:h + 1].to_broadcast([P, P]),
                                       mT[:, b % 2, :], start=False, stop=(j == HPG - 1))
                    mm.then_inc(st_ps, 1)

                def values(u):
                    b, g = divmod(u, GROUPS)
                    pe.wait_ge(keep_done, UNITS * c + u + 1)
                    if g == 0:
                        pe.wait_ge(vpad_ready, NB * c + b + 1)
                        if b == 0:
                            pe.wait_ge(max_done, UNITS * c + SECOND_BANK[-1] + 1)
                        wait(pe, on_ready, NB * c + b)
                    for j in range(HPG):
                        h = HPG * g + j
                        half = h // 8
                        mm = pe.matmul(cols_of(pO, half), PT[:, u % 2, j * P:(j + 1) * P],
                                       Vpad[:, b % 2, h, :], start=(h % 8 == 0), stop=(h % 8 == 7))
                    mm.then_inc(pv_ps, 1)

                def o_T(b):
                    pe.wait_ge(on_ready, NB * c + b + 1)
                    take_G(ot_ready, NB * c + b + 1)
                    pe.transpose(pG[:, 0:P], On[:, :], identf[:, :]).then_inc(ot_ps, 1)

                def project(b):
                    take_G(x2_done, NB * c + b + 1)
                    pe.matmul(pG[:, 0:P], OT[:, :], wo[:, :], start=True, stop=True).then_inc(wo_ps, 1)

                def third_T(b):
                    pe.wait_ge(x3n_ready, NB * c + b + 1)
                    take_G(x3T_ready, NB * c + b + 1)
                    pe.transpose(pG[:, 0:P], x3n[:, :], identf[:, :]).then_inc(x3T_ps, 1)

                scores(0)
                step(12)
                scores(1)
                scores(2)
                step(13)
                scores(3)
                step(14)
                maxima_T(0)
                scores(4)
                for u in range(UNITS):
                    b, g = divmod(u, GROUPS)
                    scores_T(u)
                    if u + AHEAD < UNITS:
                        scores(u + AHEAD)
                    if g == 3 and b + 1 < NB:
                        maxima_T(b + 1)
                    if g == 0 and b >= 2:
                        third_T(b - 2)
                    if g == 1 and b >= 1:
                        o_T(b - 1)
                    step(A_STEPS + u, None if u == 0 else lambda: values(u - 1))
                    if g == 1 and b >= 1:
                        project(b - 1)
                values(UNITS - 1)
                third_T(NB - 2)
                step(31)
                if not last:
                    first_T(c + 1)
                o_T(NB - 1)
                step(32)
                if not last:
                    context_T(c + 1)
                project(NB - 1)
                step(33)
                if not last:
                    self_queries(c + 1)
                    self_values(c + 1)
                third_T(NB - 1)
                if experts:
                    out_T(p)
                pe.wait_ge(x3T_ready, NB * (c + 1))
                take_G(lg_copied, c + 1)
                for b in range(NB):
                    mm = pe.matmul(pG[:, b * EXPERTS:(b + 1) * EXPERTS], cols_of(x3T, b), gw[:, :],
                                   start=True, stop=True)
                mm.then_inc(lg_ps, 1)

            pe.wait_ge(ident_ready, 1)
            pe.wait_ge(wts_in, 16 * 9)
            pe.wait_ge(rows_in, 16 * 5)
            for i in range(3):
                mm = pe.transpose(cols_of(pH0, i), Gb[:, 0, i * P:(i + 1) * P], identf[:, :])
            mm.then_inc(setup_T, 1)
            pe.wait_ge(setup_cp, 1)
            pe.matmul(pH1[:, 0:P], Gb[:, 1, P:2 * P], Gb[:, 1, 2 * P:3 * P], start=True,
                      stop=True).then_inc(aqk_ps, 1)
            pe.wait_ge(cast_done, 1)
            first_T(0)
            context_T(0)
            pe.wait_ge(aqk_ready, 1)
            self_queries(0)
            self_values(0)
            body(0, False, False)
            pe.wait_ge(w_lo, 2 * EXPERTS)
            body(1, False, True)
            with pe.Fori(2, CHUNKS - 1) as c:
                last_G[0], last_G[1] = lg_copied, c
                body(c, False, True)
            last_G[0], last_G[1] = lg_copied, CHUNKS - 1
            body(CHUNKS - 1, True, True)
            gates_T(CHUNKS - 1)
            for n in range(STEPS + LAG):
                expert_step(CHUNKS - 1, n)
            out_T(CHUNKS - 1)


_INS = ['x', 'ctx_1024', 'L0_attn_W_query', 'L0_attn_W_key', 'L0_attn_W_value', 'L0_xattn_w_q', 'L0_xattn_b_q',
        'L0_xattn_w_k', 'L0_xattn_b_k', 'L0_xattn_w_v', 'L0_xattn_b_v', 'L0_xattn_w_o', 'L0_xattn_b_o',
        'L0_ffn_gate_w', 'L0_ffn_w1', 'L0_ffn_b1', 'L0_ffn_w2', 'L0_ffn_b2']


def kernel(**inputs):
    import numpy as _np
    import concourse.bacc as _bacc
    from concourse import mybir as _mybir
    from concourse.bass_utils import run_bass_kernel_spmd as _run

    nc = _bacc.Bacc("TRN2", target_bir_lowering=False, num_devices=1)
    arrays, args = {}, []
    for name in _INS:
        a = _np.ascontiguousarray(inputs[name])
        arrays[f"in_{name}_dram"] = a
        args.append(nc.dram_tensor(f"in_{name}_dram", a.shape, _mybir.dt.from_np(a.dtype), kind="ExternalInput").ap())
    out = nc.dram_tensor("out_0_dram", inputs['x'].shape, _mybir.dt.float32, kind="ExternalOutput").ap()
    decoder_layer(nc, *args, out)
    r = _run(nc, [arrays], core_ids=[0])
    return r.results[0]["out_0_dram"]
```

```python
from contextlib import ExitStack

import concourse.bass as bass
from concourse import mybir

F32 = mybir.dt.float32
F32R = mybir.dt.float32r
BF16 = mybir.dt.bfloat16
U32 = mybir.dt.uint32
ALU = mybir.AluOpType
ACT = mybir.ActivationFunctionType
AX_X = mybir.AxisListType.X

P = 128
NB = 4
TOK = NB * P
HEADS = 16
DH = P // HEADS
GROUPS = 4
HPG = HEADS // GROUPS
UNITS = NB * GROUPS
EXPERTS = 8
KF = 4
STEPS = EXPERTS * KF
RING = 3
LAG = 2
AHEAD = 7
MASKED = -1e30
EPS = 1e-5
SECOND_BANK = (1, 3, 5)
W_STEPS = tuple(range(9, 17)) + tuple(range(24, 32))
NORM_UNIT = 1
APART = (0, 2)
GATES_STEP = 3
A_STEPS = 17
BARE_UNITS = (14, 15)


def wait(eng, sem, value):
    if not isinstance(value, int) or value > 0:
        eng.wait_ge(sem, value)


def step_of(u):
    return None if u in BARE_UNITS else A_STEPS + u - sum(v < u for v in BARE_UNITS)


def second_on(c):
    return not isinstance(c, int) or c >= 2


def before(p, n, ring):
    return STEPS * p + max(n - ring + 1, 0)


def decoder_layer(nc, x, ctx_in, Wq_s, Wk_s, Wv_s, w_q, b_q, w_k, b_k, w_v, b_v, w_o, b_o,
                  gate_w, w1, b1, w2, b2, out):
    B = x.shape[0]
    CHUNKS = B // NB
    SCALE_S = float(P) ** -0.5
    SCALE_X = float(DH) ** -0.5
    x_v = x.rearrange("(c b) p d -> c p b d", b=NB)
    ctx_v = ctx_in.rearrange("(c b) p d -> c p b d", b=NB)
    out_v = out.rearrange("(c b) p d -> c p b d", b=NB)

    with ExitStack() as stack:
        def sb(name, shape, dt=F32):
            return stack.enter_context(nc.sbuf_tensor(name, shape, dt))

        def sem(name):
            return stack.enter_context(nc.semaphore(name))

        identf = sb("identf", [P, P])
        identb = sb("identb", [P, P], BF16)
        maskb = sb("maskb", [P, P], BF16)
        ones_rows = sb("ones_rows", [P, 1])
        expert_rows = sb("expert_rows", [P, EXPERTS], F32R)
        q_hi_sel = sb("q_hi_sel", [P, GROUPS, P], F32R)
        q_lo_sel = sb("q_lo_sel", [P, GROUPS, P], F32R)
        k_hi_sel = sb("k_hi_sel", [P, GROUPS, P], F32R)
        k_lo_sel = sb("k_lo_sel", [P, GROUPS, P], F32R)
        minus_half = sb("minus_half", [P, NB])
        expert_no = sb("expert_no", [P, EXPERTS])
        Aqk = sb("Aqk", [P, P])
        wvs = sb("wvs", [P, P])
        wqx = sb("wqx", [P, P])
        wkx = sb("wkx", [P, P])
        wvx = sb("wvx", [P, P])
        wo = sb("wo", [P, P])
        gw = sb("gw", [P, EXPERTS])
        cols = sb("cols", [P, 64])
        bv = sb("bv", [P, P])
        bo = sb("bo", [P, P])
        w1_hi = sb("w1_hi", [P, EXPERTS, TOK], F32R)
        w1_lo = sb("w1_lo", [P, EXPERTS, TOK], F32R)
        w2_hi = sb("w2_hi", [P, EXPERTS, KF, P], F32R)
        w2_lo = sb("w2_lo", [P, EXPERTS, KF, P], F32R)
        B1, B2, GW, BQ, BK = 0, STEPS, STEPS + 8, STEPS + 16, STEPS + 17
        X = sb("X", [P, 2, NB, P])
        C = sb("C", [P, NB, P])
        xn = sb("xn", [P, NB, P])
        PTs = xn
        xnT = sb("xnT", [P, TOK])
        cT = sb("cT", [P, TOK])
        Vs = C
        PT = sb("PT", [P, 2, TOK])
        Ps, GT = PT[:, 0, :], PT[:, 1, :]
        V4 = sb("V4", [P, NB, P])
        x3T = V4[:, :, :].rearrange("p b n -> p (b n)")
        qk_hi = sb("qk_hi", [P, TOK], F32R)
        qk_lo = sb("qk_lo", [P, TOK], F32R)
        Kst = sb("Kst", [P, GROUPS, TOK], F32R)
        Qst = sb("Qst", [P, GROUPS, TOK], F32R)
        Kbd = sb("Kbd", [P, 2, GROUPS, HPG, P], F32R)
        Qbd = sb("Qbd", [P, 2, GROUPS, HPG, P], F32R)
        Vpad = sb("Vpad", [P, 2, HEADS, P])
        smx = sb("smx", [P, NB])
        nmx = sb("nmx", [P, NB])
        sden = sb("sden", [P, NB])
        srden = sb("srden", [P, NB])
        mx = sb("mx", [P, 2, HEADS])
        mcol = sb("mcol", [P, HPG, 2, GROUPS])
        mT = sb("mT", [P, P], F32R)
        rden = sb("rden", [P, HEADS])
        On = sb("On", [P, P])
        OT = sb("OT", [P, P])
        x3n = OT
        st1 = sb("st1", [P, NB, 6])
        mv1 = sb("mv1", [P, NB, 2])
        ve1 = sb("ve1", [P, NB])
        rs1 = sb("rs1", [P, NB])
        st3 = sb("st3", [P, 6])
        mv3 = sb("mv3", [P, 2])
        ve3 = sb("ve3", [P, 1])
        rs3 = sb("rs3", [P, 1])
        x3_hi = sb("x3_hi", [P, 2, TOK], F32R)
        x3_lo = sb("x3_lo", [P, 2, TOK], F32R)
        h_hi = sb("h_hi", [P, RING, TOK], F32R)
        h_lo = sb("h_lo", [P, RING, TOK], F32R)
        work = sb("work", [P, 7 + 2, TOK])
        h_full, Gb, yt, yacc = work[:, 0:RING, :], work[:, 3:5, :], work[:, 5, :], work[:, 6, :]
        x2 = work[:, 7:9, :].rearrange("p a (b d) -> p a b d", b=NB)
        w_stage = work[:, 0:EXPERTS, :]
        lg = sb("lg", [P, NB, EXPERTS])
        ex = sb("ex", [P, NB, EXPERTS])
        top = sb("top", [P, NB, 8])
        topi = sb("topi", [P, NB, 8], U32)
        topf = sb("topf", [P, NB, 8])
        is1 = sb("is1", [P, NB, EXPERTS])
        is2 = sb("is2", [P, NB, EXPERTS])
        gden = sb("gden", [P, NB])
        grden = sb("grden", [P, NB])
        gate = sb("gate", [P, NB, EXPERTS])
        gcol = sb("gcol", [P, P + (NB - 1) * 2 * EXPERTS])
        gT = sb("gT", [P, TOK], F32R)

        def pb(name):
            return stack.enter_context(nc.psum_tensor(name, [P, TOK], F32))

        pS, pT0, pT1, pO, pG, pH0, pH1, pY = (pb(n) for n in ("pS", "pT0", "pT1", "pO", "pG", "pH0", "pH1", "pY"))
        pT = (pT0, pT1)
        pH = (pH0, pH1)

        zeroed, ident_ready, selected, bd_zeroed, rows_in, qk_in, wts_in, w1_in = (
            sem(n) for n in ("zeroed", "ident_ready", "selected", "bd_zeroed", "rows_in", "qk_in", "wts_in", "w1_in"))
        cast_done, setup_T, setup_cp, aqk_ps, aqk_ready, w_hi, w_lo, vpad_init, sel_step = (
            sem(n) for n in ("cast_done", "setup_T", "setup_cp", "aqk_ps", "aqk_ready", "w_hi", "w_lo", "vpad_init", "sel_step"))
        ones_step = sem("ones_step")
        w2_in = (sem("w2_in0"), sem("w2_in1"))
        x_in, c_in, out_done = sem("x_in"), sem("c_in"), sem("out_done")
        m_in = sem("m_in")
        kbd_in = (sem("kbd_in0"), sem("kbd_in1"))
        qbd_in = (sem("qbd_in0"), sem("qbd_in1"))
        (ln_stat, ln_agg, ln_ve, ln_rstd, xn_ready, xT_ps, cT_ps, g_ps, vs_ps, k_ps, vx_ps, ss_ps, st_kps,
         xnT_ready, cT_ready, gt_ready, vs_ready, khi_ready, klo_ready, vx_ready, smax_done, nmx_ready, p_ready,
         kst_a, kst_d, pt_ps, pts_ready, pvs_ps, srden_done, x1_done, x1b_ready, q_ps, qst_ps, qst_a, qst_d) = (
            sem(n) for n in (
                "ln_stat", "ln_agg", "ln_ve", "ln_rstd", "xn_ready", "xT_ps", "cT_ps", "g_ps", "vs_ps", "k_ps",
                "vx_ps", "ss_ps", "kst_ps", "xnT_ready", "cT_ready", "gt_ready", "vs_ready", "qkhi_ready",
                "qklo_ready", "vx_ready", "smax_done", "nmx_ready", "p_ready", "kst_a", "kst_d", "pt_ps",
                "pts_ready", "pvs_ps", "srden_done", "x1_done", "x1b_ready", "q_ps", "qst_ps", "qst_a", "qst_d"))
        kst_ps, qkhi_ready, qklo_ready = st_kps, khi_ready, klo_ready
        (s_ps, max_done, m_hi, mcol_ready, mT_ps, mT_ready, st_ps, exp_done, keep_done, vpad_ready, pv_ps,
         o_rec, on_ready, ot_ps, ot_ready, wo_ps, x2_done, st3_done, mv3_done, ve3_done, rs3_done, x3n_ready,
         x3T_ps, x3hi_ready, x3T_ready, x3_ready) = (
            sem(n) for n in (
                "s_ps", "max_done", "m_hi", "mcol_ready", "mT_ps", "mT_ready", "st_ps", "exp_done", "keep_done",
                "vpad_ready", "pv_ps", "o_rec", "on_ready", "ot_ps", "ot_ready", "wo_ps", "x2_done", "st3_done",
                "mv3_done", "ve3_done", "rs3_done", "x3n_ready", "x3T_ps", "x3hi_ready", "x3T_ready", "x3_ready"))
        (lg_ps, lg_copied, top_done, topi_done, ex_in_done, ex_done, topf_done, gate_step, gcol_ready, gT_ps,
         gT_ready, gb_ps, gb_ready, up_ps, relu_done, lo_ready, dn_ps, y_scaled, y_added, oT_ps, out_ready) = (
            sem(n) for n in (
                "lg_ps", "lg_copied", "top_done", "topi_done", "ex_in_done", "ex_done", "topf_done", "gate_step",
                "gcol_ready", "gT_ps", "gT_ready", "gb_ps", "gb_ready", "up_ps", "relu_done", "lo_ready", "dn_ps",
                "y_scaled", "y_added", "oT_ps", "out_ready"))

        block = stack.enter_context(nc.Block())

        def wait_apart(eng, sem, value):
            if not isinstance(value, int):
                value = eng.to_reg(value)
                eng.wait_ge(selected, 1)
            wait(eng, sem, value)

        def X_of(c):
            return X[:, bass.ds(c % 2, 1), :, :].rearrange("p a b d -> p (a b) d")

        def Y_of(p, e):
            return pO if isinstance(p, int) and p == CHUNKS - 1 and e % 2 else pY

        def cols_of(t, b):
            return t[:, b * P:(b + 1) * P]

        def tiles(t):
            return t[:, :].rearrange("p (b n) -> p b n", b=NB)

        @block.sync
        def _(sp):
            sp.dma_start(X[:, 0, :, :], x_v[0]).then_inc(x_in, 16)
            for i, src in enumerate((Wq_s, Wk_s)):
                sp.dma_start(Gb[:, 0, i * P:(i + 1) * P], src).then_inc(qk_in, 16)
            sp.wait_ge(zeroed, 1)
            small = Gb[:, 0, 2 * P:3 * P]
            rows = ((B1, b1.rearrange("e (k p) -> (e k) p", p=P)), (B2, b2), (GW, gate_w),
                    (BQ, b_q.rearrange("(a n) -> a n", a=1)), (BK, b_k.rearrange("(a n) -> a n", a=1)))
            for r, src in rows:
                sp.dma_start(small[r:r + src.shape[0], :], src).then_inc(rows_in, 16)
            sp.dma_start(C[:, :, :], ctx_v[0]).then_inc(c_in, 16)
            for dst, src in ((wvs, Wv_s), (wkx, w_k), (wvx, w_v), (wqx, w_q), (wo, w_o),
                             (bv, b_v.partition_broadcast(P)), (bo, b_o.partition_broadcast(P))):
                sp.dma_start(dst[:, :], src).then_inc(wts_in, 16)
            sp.wait_ge(cast_done, 1)
            sp.wait_ge(aqk_ps, 1)
            sp.dma_start(w_stage, w1.rearrange("e h f -> h e f")).then_inc(w1_in, 16)

            def spread(bd, st, rows, slot, b, done):
                for j in range(HPG):
                    sp.dma_start(bd[32 * j:32 * j + rows, slot, :, j, :].bitcast(F32),
                                 st[32 * j:32 * j + rows, :, b * P:(b + 1) * P].bitcast(F32)).then_inc(done[slot], 16)

            def maxima(c, b):
                wait_apart(sp, mT_ready, NB * c + b + 1)
                for j in range(HPG):
                    r = 32 * j + 3 * DH
                    sp.dma_start(Qbd[r:r + 2, b % 2, :, j, :].bitcast(F32),
                                 mT[2 * GROUPS * j:2 * GROUPS * (j + 1), :].bitcast(F32)).then_inc(m_in, 16)

            def transfers(c, last, experts):
                def second_weights(first, end):
                    for e in range(first, end) if not experts else ():
                        sp.wait_ge(w_lo, e + 1)
                        sp.dma_start(w_stage[:, e, :].rearrange("p (k n) -> p k n", k=KF),
                                     w2[e].rearrange("(k p) h -> p k h", p=P)).then_inc(w2_in[e // 4], 16)

                if not last:
                    wait_apart(sp, x2_done, NB * c)
                    sp.dma_start(X_of(c + 1), x_v[bass.ds(c + 1, 1)].rearrange("a p b d -> p (a b) d")).then_inc(x_in, 16)
                if second_on(c):
                    store(c - 2)
                if not experts:
                    sp.wait_ge(bd_zeroed, 1)
                wait_apart(sp, kst_a, 2 * c + 2)
                wait_apart(sp, kst_d, 2 * c + 2)
                wait_apart(sp, s_ps, UNITS * c)
                spread(Kbd, Kst, 32, 0, 0, kbd_in)
                spread(Kbd, Kst, 32, 1, 1, kbd_in)
                wait_apart(sp, pvs_ps, c + 1)
                if not last:
                    sp.dma_start(C[:, :, :], ctx_v[bass.ds(c + 1, 1)].rearrange("a p b d -> p (a b) d")).then_inc(c_in, 16)
                wait_apart(sp, qst_a, 2 * c + 2)
                wait_apart(sp, qst_d, 2 * c + 2)
                wait_apart(sp, st_ps, UNITS * c)
                spread(Qbd, Qst, 3 * DH, 0, 0, qbd_in)
                maxima(c, 0)
                wait_apart(sp, s_ps, UNITS * c + 4)
                spread(Kbd, Kst, 32, 0, 2, kbd_in)
                spread(Qbd, Qst, 3 * DH, 1, 1, qbd_in)
                wait_apart(sp, s_ps, UNITS * c + 8)
                spread(Kbd, Kst, 32, 1, 3, kbd_in)
                maxima(c, 1)
                second_weights(0, 4)
                wait_apart(sp, st_ps, UNITS * c + 4)
                spread(Qbd, Qst, 3 * DH, 0, 2, qbd_in)
                maxima(c, 2)
                second_weights(4, EXPERTS)
                wait_apart(sp, st_ps, UNITS * c + 8)
                spread(Qbd, Qst, 3 * DH, 1, 3, qbd_in)
                maxima(c, 3)

            def store(p):
                wait_apart(sp, out_ready, p + 1)
                src = x2[:, bass.ds((p + 1) % 2, 1), :, :].rearrange("p a b d -> p (a b) d")
                sp.dma_start(out_v[bass.ds(p, 1)].rearrange("a p b d -> p (a b) d"), src).then_inc(out_done, 16)

            transfers(0, False, False)
            transfers(1, False, True)
            with sp.Fori(2, CHUNKS - 1) as c:
                transfers(c, False, True)
            transfers(CHUNKS - 1, True, True)
            store(CHUNKS - 2)
            store(CHUNKS - 1)
            sp.wait_ge(out_done, 16 * CHUNKS)

        @block.gpsimd
        def _(pool):
            pool.memset(Gb[:, 0, 2 * P:3 * P], 0.0).then_inc(zeroed, 1)
            pool.memset(identf[:, :], 0.0).then_inc(sel_step, 1)
            pool.wait_ge(sel_step, 1)
            pool.affine_select(out=identf[:, :], in_=identf[:, :], compare_op=ALU.not_equal, fill=1.0, base=0,
                               pattern=[[-1, P]], channel_multiplier=1).then_inc(ident_ready, 1)
            pool.memset(maskb[:, :], 0.0)
            pool.memset(Gb[:, 1, 0:EXPERTS], 0.0)
            pool.memset(PT[:, :, :], 0.0)
            pool.memset(yacc[:, :], 0.0)
            pool.memset(V4[:, :, :], 0.0)
            pool.memset(minus_half[:, :], -0.5)
            for e in range(EXPERTS):
                pool.memset(expert_no[:, e:e + 1], float(e))
            pool.memset(gcol[:, :], 0.0)
            pool.memset(srden[:, :], 0.0).then_inc(sel_step, 1)
            pool.wait_ge(sel_step, 2)
            pool.affine_select(out=maskb[:, :], in_=maskb[:, :], compare_op=ALU.is_ge, fill=MASKED, base=0,
                               pattern=[[-1, P]], channel_multiplier=1)
            pick = ((PT[:, 0, :], slice(0, 2)), (PT[:, 1, :], slice(2, 3)),
                    (yacc[:, :], slice(0, 3, 2)),
                    (V4[:, :, :].rearrange("p b n -> p (b n)"), slice(1, 2)))
            for t, copies in pick:
                v = t.rearrange("p (h i d) -> p h i d", h=HEADS, d=DH)[:, :, copies, :]
                along = [[-DH, HEADS], [0, 2], [-1, DH]] if v.shape[2] == 2 else [[-DH, HEADS], [-1, DH]]
                v = v if v.shape[2] == 2 else v.rearrange("p h i d -> p h (i d)")
                pool.affine_select(out=v, in_=v, compare_op=ALU.not_equal, fill=1.0, base=0,
                                   pattern=along, channel_multiplier=1)
            def power(ve, rs, n):
                return pool.tensor_tensor(rs, ve, minus_half[:, 0:n], ALU.pow)

            def norm_power(i):
                pool.wait_ge(ln_ve, i)
                power(ve1[:, :], rs1[:, :], NB).then_inc(ln_rstd, 1)

            norm_power(1)
            for base in (0, -EXPERTS):
                v = Gb[:, 1, 0:EXPERTS]
                pool.affine_select(out=v, in_=v, compare_op=ALU.not_equal, fill=1.0, base=base,
                                   pattern=[[-1, EXPERTS]], channel_multiplier=1).then_inc(sel_step, 1)
                if base == 0:
                    pool.wait_ge(sel_step, 3)
            pool.wait_ge(sel_step, 4)
            pool.memset(smx[:, :], 0.0).then_inc(selected, 1)

            def fill_vpad(c, b):
                wait_apart(pool, pv_ps, UNITS * c + GROUPS * (b - 1))
                wait_apart(pool, vx_ready, c + 1)
                w = P + 2 * DH
                for half in range(2):
                    flat = Vpad[:, b % 2, 8 * half:8 * half + 8, :].rearrange("p h n -> p (h n)")
                    vals = V4[:, b, 64 * half:64 * half + 64].rearrange("p (h d) -> p h d", d=DH)
                    pool.tensor_copy(flat[:, 0:7 * w].rearrange("p (h n) -> p h n", n=w)[:, :, 0:DH], vals[:, 0:7, :])
                    ins = pool.tensor_copy(flat[:, 7 * w:7 * w + DH], vals[:, 7, :])
                ins.then_inc(vpad_ready, 1)

            def keep_causal(c, u):
                wait_apart(pool, exp_done, UNITS * c + u + 1)
                v = PT[:, u % 2, :].rearrange("p (h q) -> p h q", h=HPG)
                pool.affine_select(out=v, in_=v, compare_op=ALU.is_ge, fill=0.0, base=0,
                                   pattern=[[0, HPG], [1, P]], channel_multiplier=-1).then_inc(keep_done, 1)

            def expert_step(p, n):
                e, r = divmod(n - 6, KF)
                if r == 0 and 1 <= e < EXPERTS:
                    pool.wait_ge(y_scaled, EXPERTS * p + e + 1)
                    pool.tensor_tensor(yacc[:, :], yacc[:, :], yt[:, :], ALU.add).then_inc(y_added, 1)
                    pool.wait_ge(y_added, (EXPERTS - 1) * p + e)

            def third_power(c, b):
                pool.wait_ge(ve3_done, NB * c + b + 1)
                power(ve3[:, :], rs3[:, :], 1).then_inc(rs3_done, 1)

            def body(c, last, experts):
                p = c - 1

                def step(n):
                    if experts:
                        expert_step(p, n)

                for n in range(7):
                    step(n)
                norm_power(2 * c + 2)
                if not experts:
                    pool.wait_ge(vpad_init, 2)
                fill_vpad(c, 0)
                fill_vpad(c, 1)
                pool.wait_ge(xn_ready, 2 * c + 2)
                for b in range(NB):
                    ins = pool.tensor_tensor(X_of(c)[:, b, :], X_of(c)[:, b, :], bo[:, :], ALU.add)
                ins.then_inc(x1b_ready, 1)
                for n in range(7, A_STEPS):
                    step(n)
                for u in range(UNITS):
                    b, g = divmod(u, GROUPS)
                    keep_causal(c, u)
                    if g == 1 and 2 <= b + 1 < NB:
                        fill_vpad(c, b + 1)
                    if g == 2 and b >= 1:
                        third_power(c, b - 1)
                    if u == NORM_UNIT + 1 and not last:
                        norm_power(2 * c + 3)
                    if step_of(u):
                        step(step_of(u))
                step(31)
                step(32)
                third_power(c, NB - 1)
                step(33)
                step(34)

            pool.memset(Kbd[:, :, :, :, :].bitcast(F32), 0.0)
            pool.memset(Qbd[:, :, :, :, :].bitcast(F32), 0.0).then_inc(bd_zeroed, 1)
            body(0, False, False)
            body(1, False, True)
            with pool.Fori(2, CHUNKS - 1) as c:
                body(c, False, True)
            body(CHUNKS - 1, True, True)
            for n in range(STEPS + 3):
                expert_step(CHUNKS - 1, n)

        @block.scalar
        def _(act):
            def copy(dst, src):
                return act.activation(dst, src, ACT.Copy)

            def expert_step(p, n, between=None):
                if n < STEPS:
                    act.wait_ge(up_ps, STEPS * p + n + 1)
                    wait(act, dn_ps, before(p, n, RING))
                    act.activation(h_hi[:, n % RING, :], pH[n % 2][:, :], ACT.Relu, bias=cols[:, B1 + n:B1 + n + 1])
                    wait(act, lo_ready, before(p, n, RING))
                    act.activation(h_full[:, n % RING, :], pH[n % 2][:, :], ACT.Relu,
                                   bias=cols[:, B1 + n:B1 + n + 1]).then_inc(relu_done, 1)
                if between is not None:
                    between()
                if n % KF == 3 and n < STEPS:
                    e = n // KF
                    act.wait_ge(gb_ps, EXPERTS * p + e + 1)
                    wait(act, y_scaled, EXPERTS * p + max(e - 1, 0))
                    copy(Gb[:, e % 2, :], pG[:, :]).then_inc(gb_ready, 1)

            def gates_T(p):
                act.wait_ge(gT_ps, p + 1)
                wait(act, gb_ps, EXPERTS * p)
                copy(gT[:, :], pG[:, :]).then_inc(gT_ready, 1)

            def stack_evac(dst, ps, done, c):
                for g in (0, 2):
                    act.wait_ge(ps, GROUPS * c + g + 1)
                    if dst is Kst:
                        act.activation(dst[:, g, :], pT0[:, :], ACT.Identity, bias=ones_rows[:, :]).then_inc(done, 1)
                    else:
                        copy(dst[:, g, :], pT0[:, :]).then_inc(done, 1)
                    yield

            def third_T(c, b):
                act.wait_ge(x3T_ps, NB * c + b + 1)
                wait(act, oT_ps, c - 1)
                copy(x3_hi[:, bass.ds(c % 2, 1), b * P:(b + 1) * P].rearrange("p a n -> p (a n)"),
                     pG[:, 0:P]).then_inc(x3hi_ready, 1)

            def first_T(c):
                act.wait_ge(xT_ps, 2 * c + 1)
                copy(xnT[:, :], pT0[:, :]).then_inc(xnT_ready, 1)

            def gates_exp(p):
                act.wait_ge(ex_in_done, p + 1)
                act.activation(ex[:, :, :], ex[:, :, :], ACT.Exp).then_inc(ex_done, 1)

            def weights_hi(n):
                e = n % EXPERTS
                act.wait_ge(*((w1_in, 16) if n < EXPERTS else (w2_in[e // 4], 16 * 4)))
                dst = w1_hi[:, e] if n < EXPERTS else w2_hi[:, e].rearrange("p k n -> p (k n)")
                copy(dst, w_stage[:, e, :]).then_inc(w_hi, 1)

            def body(c, last, experts):
                p = c - 1

                def step(n):
                    if experts:
                        expert_step(p, n)
                    elif n in W_STEPS:
                        weights_hi(W_STEPS.index(n))

                act.wait_ge(g_ps, c + 1)
                copy(GT, pS[:, :]).then_inc(gt_ready, 1)
                act.wait_ge(k_ps, c + 1)
                wait(act, qst_ps, GROUPS * c)
                act.activation(qk_hi[:, :], pT0[:, :], ACT.Identity, bias=cols[:, BK:BK + 1]).then_inc(qkhi_ready, 1)
                if experts:
                    gates_exp(p)
                step(0)
                kst = stack_evac(Kst, kst_ps, kst_a, c)
                wait(act, st_ps, UNITS * c)
                next(kst)
                for b in range(NB):
                    act.wait_ge(nmx_ready, c + 1)
                    ins = act.activation(cols_of(Ps, b), cols_of(pS, b), ACT.Exp, bias=nmx[:, b:b + 1],
                                         scale=SCALE_S, accum_out=sden[:, b:b + 1])
                ins.then_inc(p_ready, 1)
                step(1)
                step(2)
                next(kst)
                if experts:
                    gates_T(p)
                act.wait_ge(pt_ps, c + 1)
                copy(PTs[:, :, :].rearrange("p b n -> p (b n)"), pO[:, :]).then_inc(pts_ready, 1)
                for n in range(3, 9):
                    step(n)
                act.wait_ge(xT_ps, 2 * c + 2)
                copy(xnT[:, :], pO[:, :]).then_inc(xnT_ready, 1)
                step(9)
                act.wait_ge(q_ps, c + 1)
                act.wait_ge(kst_ps, GROUPS * (c + 1))
                act.activation(qk_hi[:, :], pT0[:, :], ACT.Identity, bias=cols[:, BQ:BQ + 1]).then_inc(qkhi_ready, 1)
                step(10)
                qst = stack_evac(Qst, qst_ps, qst_a, c)
                wait(act, s_ps, UNITS * c)
                next(qst)
                step(11)
                next(qst)
                step(12)
                step(13)

                def m_T(b):
                    act.wait_ge(mT_ps, NB * c + b + 1)
                    wait(act, m_in, 16 * HPG * (NB * c + b))
                    rows = 2 * HEADS
                    copy(mT[0:rows, :], pG[0:rows, 0:P]).then_inc(mT_ready, 1)

                def o_T(b):
                    act.wait_ge(ot_ps, NB * c + b + 1)
                    wait(act, x3T_ps, NB * c + b)
                    copy(OT[:, :], pG[:, 0:P]).then_inc(ot_ready, 1)

                m_T(0)
                step(14)
                step(15)
                step(16)
                for u in range(UNITS):
                    b, g = divmod(u, GROUPS)
                    act.wait_ge(st_ps, UNITS * c + u + 1)
                    wait(act, pv_ps, UNITS * c + u - 1)
                    act.activation(PT[:, u % 2, :], pT[u % 2][:, :], ACT.Exp, scale=SCALE_X).then_inc(exp_done, 1)
                    if g == 0 and b >= 2:
                        third_T(c, b - 2)
                    if g == 1 and b + 1 < NB:
                        m_T(b + 1)
                    if step_of(u):
                        step(step_of(u))
                    if g == 1 and b >= 1:
                        o_T(b - 1)

                def between():
                    third_T(c, NB - 2)
                    o_T(NB - 1)

                if experts:
                    expert_step(p, 31, between)
                else:
                    step(31)
                    between()
                if not last:
                    first_T(c + 1)
                third_T(c, NB - 1)

            act.wait_ge(sel_step, 2)
            act.activation(srden[:, 0:1], minus_half[:, 0:1], ACT.Exp)
            first_T(0)
            act.wait_ge(cast_done, 1)
            body(0, False, False)
            body(1, False, True)
            with act.Fori(2, CHUNKS - 1) as c:
                body(c, False, True)
            body(CHUNKS - 1, True, True)
            gates_exp(CHUNKS - 1)
            for n in range(STEPS):
                if n == GATES_STEP:
                    gates_T(CHUNKS - 1)
                expert_step(CHUNKS - 1, n)

        @block.vector
        def _(dve):
            def norm_stats(src, i):
                for b in range(NB):
                    ins = dve.bn_stats(st1[:, b, :], src[:, b, :])
                ins.then_inc(ln_stat, 1)

            def norm_aggregate(i):
                wait_apart(dve, ln_stat, i)
                for b in range(NB):
                    ins = dve.bn_aggr(mv1[:, b, :], st1[:, b, :])
                ins.then_inc(ln_agg, 1)
                dve.wait_ge(ln_agg, i)
                dve.tensor_scalar(ve1[:, :], mv1[:, :, 1], EPS, None, ALU.add).then_inc(ln_ve, 1)

            def norm_apply(src, i, batches=range(NB)):
                dve.wait_ge(ln_rstd, i)
                for b in batches:
                    ins = dve.tensor_scalar(xn[:, b, :], src[:, b, :], mv1[:, b, 0:1], rs1[:, b:b + 1],
                                            ALU.subtract, ALU.mult)
                if b == NB - 1:
                    ins.then_inc(xn_ready, 1)

            def vpad_constants():
                dve.memset(Vpad[:, :, :, :], 0.0).then_inc(vpad_init, 1)
                dve.wait_ge(vpad_init, 1)
                for s in range(2):
                    for h in range(HEADS):
                        c0 = 2 * DH * (h % 8) + DH
                        ins = dve.memset(Vpad[:, s, h, c0:c0 + DH], 1.0)
                ins.then_inc(vpad_init, 1)

            vpad_constants()
            dve.wait_ge(x_in, 16)
            norm_stats(X_of(0), 1)
            norm_aggregate(1)
            dve.wait_ge(setup_T, 1)
            dve.tensor_copy(Gb[:, 1, P:3 * P], pH0[:, 0:2 * P])
            dve.tensor_copy(cols[:, :], pH0[:, 2 * P:2 * P + 64])
            dve.tensor_copy(gw[:, :], pH0[:, 2 * P + GW:2 * P + GW + EXPERTS]).then_inc(setup_cp, 1)
            norm_apply(X_of(0), 1)
            dve.wait_ge(aqk_ps, 1)
            dve.tensor_copy(Aqk[:, :], pH1[:, 0:P]).then_inc(aqk_ready, 1)
            dve.wait_ge(selected, 1)
            dve.tensor_copy(identb[:, :], identf[:, :])
            spare = identf[:, :].rearrange("p (j r) -> p j r", j=HPG)[:, :, 3 * DH:3 * DH + 2]
            dve.tensor_reduce(smx[:, :], spare, AX_X, ALU.add).then_inc(ones_step, 1)
            dve.wait_ge(ones_step, 1)
            dve.tensor_reduce(ones_rows[:, :], smx[:, :], AX_X, ALU.add)
            for t, src in ((q_hi_sel, PT[:, 0, :]), (q_lo_sel, PT[:, 1, :]),
                           (k_hi_sel, yacc[:, :]),
                           (k_lo_sel, V4[:, :, :].rearrange("p b n -> p (b n)"))):
                dve.tensor_copy(t[:, :, :].rearrange("p g n -> p (g n)"), src)
            dve.tensor_copy(expert_rows[:, :], Gb[:, 1, 0:EXPERTS]).then_inc(cast_done, 1)

            def weights_lo(n):
                e = n % EXPERTS
                hi, lo = (w1_hi[:, e], w1_lo[:, e]) if n < EXPERTS else (
                    t[:, e].rearrange("p k n -> p (k n)") for t in (w2_hi, w2_lo))
                dve.wait_ge(w_hi, n + 1)
                dve.tensor_tensor(lo, w_stage[:, e, :], hi.bitcast(F32), ALU.subtract).then_inc(w_lo, 1)

            def expert_scale(p, e):
                dve.wait_ge(dn_ps, STEPS * p + KF * (e + 1))
                dve.wait_ge(gb_ready, EXPERTS * p + e + 1)
                if e == 0:
                    wait(dve, oT_ps, p)
                else:
                    wait(dve, y_added, (EXPERTS - 1) * p + e - 1)
                dve.scalar_tensor_tensor(out=(yacc if e == 0 else yt)[:, :], in0=Y_of(p, e)[:, :],
                                         scalar=cols[:, B2 + e:B2 + e + 1], in1=Gb[:, e % 2, :],
                                         op0=ALU.add, op1=ALU.mult).then_inc(y_scaled, 1)

            def expert_step(p, n):
                e, r = divmod(n - LAG - KF + 1, KF)
                last = isinstance(p, int) and p == CHUNKS - 1
                if r == 0 and e >= 0 and e not in APART and not last:
                    expert_scale(p, e)
                if n < STEPS:
                    dve.wait_ge(relu_done, STEPS * p + n + 1)
                    wait(dve, dn_ps, before(p, n, RING))
                    dve.tensor_tensor(h_lo[:, n % RING, :], h_full[:, n % RING, :], h_hi[:, n % RING, :].bitcast(F32),
                                      ALU.subtract).then_inc(lo_ready, 1)
                if r == 0 and e >= 0 and last:
                    expert_scale(p, e)

            def out_add(p):
                dve.wait_ge(oT_ps, p + 1)
                v = x2[:, bass.ds((p + 1) % 2, 1), :, :].rearrange("p a b d -> p (a b d)")
                dve.tensor_tensor(v, pG[:, :], v, ALU.add).then_inc(out_ready, 1)

            def third_x2(c, b):
                v = x2[:, bass.ds((c + 1) % 2, 1), b, :].rearrange("p a d -> p (a d)")
                dve.wait_ge(wo_ps, NB * c + b + 1)
                dve.wait_ge(x1b_ready, c + 1)
                if b == 0:
                    wait(dve, out_done, 16 * (c - 1))
                dve.tensor_tensor(v, pG[:, 0:P], X_of(c)[:, b, :], ALU.add).then_inc(x2_done, 1)
                wait_apart(dve, x2_done, NB * c + b + 1)
                dve.bn_stats(st3[:, :], v).then_inc(st3_done, 1)
                wait_apart(dve, st3_done, NB * c + b + 1)
                dve.bn_aggr(mv3[:, :], st3[:, :]).then_inc(mv3_done, 1)
                dve.wait_ge(mv3_done, NB * c + b + 1)
                dve.tensor_scalar(ve3[:, :], mv3[:, 1:2], EPS, None, ALU.add).then_inc(ve3_done, 1)

            def third_norm(c, b):
                dve.wait_ge(rs3_done, NB * c + b + 1)
                wait(dve, x3T_ps, NB * c + b)
                v = x2[:, bass.ds((c + 1) % 2, 1), b, :].rearrange("p a d -> p (a d)")
                dve.tensor_scalar(x3n[:, :], v, mv3[:, 0:1], rs3[:, :], ALU.subtract, ALU.mult).then_inc(x3n_ready, 1)

            def third_T(c, b):
                dve.wait_ge(x3T_ps, NB * c + b + 1)
                dve.wait_ge(x3hi_ready, NB * c + b + 1)
                dve.wait_ge(vpad_ready, NB * c + b + 1)
                dve.tensor_copy(x3T[:, b * P:(b + 1) * P], pG[:, 0:P]).then_inc(x3T_ready, 1)
                dve.wait_ge(x3T_ready, NB * c + b + 1)
                hi, lo = (t[:, bass.ds(c % 2, 1), b * P:(b + 1) * P].rearrange("p a n -> p (a n)") for t in (x3_hi, x3_lo))
                dve.tensor_tensor(lo, x3T[:, b * P:(b + 1) * P], hi.bitcast(F32), ALU.subtract).then_inc(x3_ready, 1)

            def gates_softmax(c):
                wait_apart(dve, lg_copied, c + 1)
                for b in range(NB):
                    ins = dve.max(top[:, b, :], lg[:, b, :])
                ins.then_inc(top_done, 1)
                dve.wait_ge(top_done, c + 1)
                dve.tensor_tensor(ex[:, :, :], lg[:, :, :], top[:, :, 0:1].to_broadcast([P, NB, EXPERTS]),
                                  ALU.subtract).then_inc(ex_in_done, 1)

            def gates_top(c):
                for b in range(NB):
                    ins = dve.max_index(topi[:, b, :], top[:, b, :], lg[:, b, :])
                ins.then_inc(topi_done, 1)
                dve.wait_ge(ex_done, c + 1)
                dve.tensor_reduce(gden[:, :], ex[:, :, :], AX_X, ALU.add).then_inc(gate_step, 1)
                dve.wait_ge(topi_done, c + 1)
                dve.tensor_copy(topf[:, :, :], topi[:, :, :]).then_inc(topf_done, 1)
                dve.wait_ge(gate_step, 7 * c + 1)
                dve.reciprocal(grden[:, :], gden[:, :]).then_inc(gate_step, 1)
                number = expert_no[:, :].unsqueeze(1).to_broadcast([P, NB, EXPERTS])
                dve.wait_ge(topf_done, c + 1)
                dve.tensor_tensor(is1[:, :, :], number, topf[:, :, 0:1].to_broadcast([P, NB, EXPERTS]), ALU.is_equal)
                dve.tensor_tensor(is2[:, :, :], number, topf[:, :, 1:2].to_broadcast([P, NB, EXPERTS]),
                                  ALU.is_equal).then_inc(gate_step, 1)
                dve.wait_ge(gate_step, 7 * c + 2)
                dve.tensor_tensor(gate[:, :, :], ex[:, :, :], grden[:, :].unsqueeze(2).to_broadcast([P, NB, EXPERTS]),
                                  ALU.mult).then_inc(gate_step, 1)
                dve.wait_ge(gate_step, 7 * c + 3)
                dve.tensor_tensor(is1[:, :, :], is1[:, :, :], is2[:, :, :], ALU.add).then_inc(gate_step, 1)
                dve.wait_ge(gate_step, 7 * c + 5)
                dve.tensor_tensor(gate[:, :, :], is1[:, :, :], gate[:, :, :], ALU.mult).then_inc(gate_step, 1)
                dve.wait_ge(gate_step, 7 * c + 6)
                both = gcol[:, 0:2 * EXPERTS * NB].rearrange("p (b n) -> p b n", b=NB)
                hi = both[:, :, 0:EXPERTS]
                wait(dve, gT_ps, c)
                dve.tensor_copy(hi.bitcast(F32R), gate[:, :, :]).then_inc(gate_step, 1)
                dve.wait_ge(gate_step, 7 * c + 7)
                dve.tensor_tensor(both[:, :, EXPERTS:2 * EXPERTS], gate[:, :, :], hi, ALU.subtract).then_inc(gcol_ready, 1)

            def context_T(c):
                dve.wait_ge(cT_ps, c + 1)
                dve.tensor_copy(cT[:, :], pT1[:, :]).then_inc(cT_ready, 1)

            def body(c, last, experts):
                p = c - 1

                def step(n):
                    if experts:
                        expert_step(p, n)
                    elif n in W_STEPS:
                        weights_lo(W_STEPS.index(n))


                def low(ps, bias, i):
                    dve.wait_ge(ps, c + 1)
                    dve.wait_ge(qkhi_ready, i)
                    dve.scalar_tensor_tensor(out=qk_lo[:, :], in0=pT0[:, :], scalar=cols[:, bias:bias + 1],
                                             in1=qk_hi[:, :].bitcast(F32), op0=ALU.add,
                                             op1=ALU.subtract).then_inc(qklo_ready, 1)

                low(k_ps, BK, 2 * c + 1)
                dve.wait_ge(ss_ps, c + 1)
                dve.tensor_reduce(smx[:, :], tiles(pS), AX_X, ALU.max).then_inc(smax_done, 1)
                dve.wait_ge(smax_done, c + 1)
                dve.tensor_scalar(nmx[:, :], smx[:, :], -SCALE_S, None, ALU.mult).then_inc(nmx_ready, 1)
                dve.wait_ge(vx_ps, c + 1)
                wait(dve, lg_ps, c)
                wait(dve, x3_ready, NB * c)
                dve.tensor_tensor(V4[:, :, :], tiles(pT1), bv[:, :].unsqueeze(1).to_broadcast([P, NB, P]),
                                  ALU.add).then_inc(vx_ready, 1)
                dve.wait_ge(vs_ps, c + 1)
                dve.tensor_copy(Vs[:, :, :].rearrange("p b n -> p (b n)"), pO[:, :]).then_inc(vs_ready, 1)
                if second_on(c):
                    out_add(c - 2)

                def stack(dst, ps, done, g):
                    dve.wait_ge(ps, GROUPS * c + g + 1)
                    if dst is Kst:
                        dve.tensor_scalar(dst[:, g, :], pT1[:, :], ones_rows[:, :], None, ALU.add).then_inc(done, 1)
                    else:
                        dve.tensor_copy(dst[:, g, :], pT1[:, :]).then_inc(done, 1)

                wait(dve, st_ps, UNITS * c)
                step(0)
                stack(Kst, kst_ps, kst_d, 1)
                if experts:
                    gates_top(p)
                step(1)
                dve.wait_ge(p_ready, c + 1)
                dve.reciprocal(srden[:, :], sden[:, :]).then_inc(srden_done, 1)
                stack(Kst, kst_ps, kst_d, 3)
                step(2)
                step(3)
                dve.wait_ge(srden_done, c + 1)
                dve.wait_ge(pvs_ps, c + 1)
                for b in range(NB):
                    ins = dve.scalar_tensor_tensor(out=X_of(c)[:, b, :], in0=cols_of(pS, b), scalar=srden[:, b:b + 1],
                                                   in1=X_of(c)[:, b, :], op0=ALU.mult, op1=ALU.add)
                ins.then_inc(x1_done, 1)
                step(4)
                if experts:
                    expert_scale(p, 0)
                wait_apart(dve, x1_done, c + 1)
                norm_stats(X_of(c), 2 * c + 2)
                step(5)
                norm_aggregate(2 * c + 2)
                step(6)
                norm_apply(X_of(c), 2 * c + 2)
                step(7)
                step(8)
                step(9)
                low(q_ps, BQ, 2 * c + 2)
                step(10)
                stack(Qst, qst_ps, qst_d, 1)
                step(11)
                stack(Qst, qst_ps, qst_d, 3)

                def unit_max(t):
                    b, g = divmod(t, GROUPS)
                    dve.wait_ge(s_ps, UNITS * c + t + 1)
                    bank = pO if t in SECOND_BANK else pS
                    dve.tensor_reduce(mx[:, b % 2, GROUPS * g:GROUPS * g + HPG], tiles(bank), AX_X,
                                      ALU.max).then_inc(max_done, 1)
                    if g == GROUPS - 1:
                        dve.wait_ge(max_done, UNITS * c + t + 1)
                        wait(dve, mT_ps, NB * c + b)
                        most = mx[:, b % 2, :].rearrange("p (g j) -> p j g", g=GROUPS)
                        dve.tensor_scalar(mcol[:, :, 0, :].bitcast(F32R), most, -1.0, None, ALU.mult).then_inc(m_hi, 1)
                        dve.wait_ge(m_hi, NB * c + b + 1)
                        dve.scalar_tensor_tensor(out=mcol[:, :, 1, :], in0=most, scalar=-1.0,
                                                 in1=mcol[:, :, 0, :], op0=ALU.mult,
                                                 op1=ALU.subtract).then_inc(mcol_ready, 1)

                def normalise(b):
                    i = NB * c + b + 1
                    heads = pO[:, 0:2 * P].rearrange("p (h n) -> p h n", h=HEADS)
                    dve.wait_ge(pv_ps, UNITS * c + GROUPS * (b + 1))
                    dve.reciprocal(rden[:, :], heads[:, :, DH]).then_inc(o_rec, 1)
                    dve.wait_ge(o_rec, i)
                    wait(dve, ot_ps, i - 1)
                    dve.tensor_tensor(On[:, :].rearrange("p (h d) -> p h d", h=HEADS), heads[:, :, 0:DH],
                                      rden[:, :].unsqueeze(2).to_broadcast([P, HEADS, DH]),
                                      ALU.mult).then_inc(on_ready, 1)

                unit_max(0)
                unit_max(1)
                step(12)
                unit_max(2)
                unit_max(3)
                if experts:
                    expert_scale(p, 2)
                unit_max(4)
                step(13)
                unit_max(5)
                step(14)
                unit_max(6)
                step(15)
                step(16)
                for u in range(UNITS):
                    b, g = divmod(u, GROUPS)
                    if u + AHEAD < UNITS:
                        unit_max(u + AHEAD)
                    if g == 0 and b >= 2:
                        third_T(c, b - 2)
                    if g == 2 and b >= 1:
                        third_x2(c, b - 1)
                    if g == 3 and b >= 1:
                        third_norm(c, b - 1)
                    if g == 0 and b >= 1:
                        normalise(b - 1)
                    if step_of(u):
                        step(step_of(u))
                    if u == NORM_UNIT and not last:
                        wait_apart(dve, x_in, 16 * (c + 2))
                        norm_stats(X_of(c + 1), 2 * c + 3)
                        norm_aggregate(2 * c + 3)
                    if u == NORM_UNIT + 1 and not last:
                        norm_apply(X_of(c + 1), 2 * c + 3, range(2))
                    if u == NORM_UNIT + 2 and not last:
                        norm_apply(X_of(c + 1), 2 * c + 3, range(2, NB))
                normalise(NB - 1)
                third_T(c, NB - 2)
                step(31)
                third_x2(c, NB - 1)
                if not last:
                    context_T(c + 1)
                step(33)
                third_norm(c, NB - 1)
                third_T(c, NB - 1)
                dve.wait_ge(lg_ps, c + 1)
                dve.tensor_copy(lg[:, :, :].rearrange("p b e -> p (b e)"),
                                pG[:, 0:NB * EXPERTS]).then_inc(lg_copied, 1)
                gates_softmax(c)

            context_T(0)
            body(0, False, False)
            body(1, False, True)
            with dve.Fori(2, CHUNKS - 1) as c:
                body(c, False, True)
            body(CHUNKS - 1, True, True)
            out_add(CHUNKS - 2)
            for n in range(STEPS + 3):
                expert_step(CHUNKS - 1, n)
                if n == 0:
                    gates_top(CHUNKS - 1)
            out_add(CHUNKS - 1)

        @block.tensor
        def _(pe):
            last_G = [None, None]

            def take_G(reader, count):
                if last_G[0] is not None:
                    wait(pe, *last_G)
                last_G[0], last_G[1] = reader, count

            def up(p, n):
                e, k = divmod(n, KF)
                if n == 0:
                    pe.wait_ge(x3_ready, NB * (p + 1))
                wait(pe, relu_done, before(p, n, 2))
                rh, rl = (t[:, bass.ds(p % 2, 1), :].rearrange("p a n -> p (a n)") for t in (x3_hi, x3_lo))
                wh, wl = w1_hi[:, e, k * P:(k + 1) * P], w1_lo[:, e, k * P:(k + 1) * P]
                pe.matmul(pH[n % 2][:, :], wh, rh, start=True, stop=False)
                pe.matmul(pH[n % 2][:, :], wh, rl, start=False, stop=False)
                pe.matmul(pH[n % 2][:, :], wl, rh, start=False, stop=True).then_inc(up_ps, 1)

            def down(p, n):
                e, k = divmod(n, KF)
                pe.wait_ge(lo_ready, STEPS * p + n + 1)
                bank = Y_of(p, e)
                if k == 0:
                    behind = isinstance(p, int) and p == CHUNKS - 1 and e > 0
                    wait(pe, y_scaled, EXPERTS * p + e - behind)
                rh, rl = h_hi[:, n % RING, :], h_lo[:, n % RING, :]
                wh, wl = w2_hi[:, e, k, :], w2_lo[:, e, k, :]
                pe.matmul(bank[:, :], wh, rh, start=(k == 0), stop=False)
                pe.matmul(bank[:, :], wl, rh, start=False, stop=False)
                pe.matmul(bank[:, :], wh, rl, start=False, stop=(k == KF - 1)).then_inc(dn_ps, 1)

            def spread_gate(p, n):
                if n % KF == 3 and n < STEPS:
                    e = n // KF
                    pe.wait_ge(gT_ready, p + 1)
                    take_G(gb_ready, EXPERTS * p + e + 1)
                    pe.matmul(pG[:, :], expert_rows[:, e:e + 1].to_broadcast([P, P]), gT[:, :],
                              start=True, stop=True).then_inc(gb_ps, 1)

            def expert_step(p, n, between=None, behind=None):
                if n < STEPS:
                    up(p, n)
                if between is not None:
                    between()
                if LAG <= n < STEPS + LAG:
                    down(p, n - LAG)
                if behind is not None:
                    behind()
                spread_gate(p, n)

            def transposes(bank, src, done):
                for b in range(NB):
                    mm = pe.transpose(cols_of(bank, b), src(b), identf[:, :])
                mm.then_inc(done, 1)

            def products(bank, lhsT, rhs, done):
                for b in range(NB):
                    mm = pe.matmul(cols_of(bank, b), lhsT(b), rhs(b), start=True, stop=True)
                mm.then_inc(done, 1)

            def gates_T(p):
                pe.wait_ge(gcol_ready, p + 1)
                take_G(gT_ready, p + 1)
                transposes(pG, lambda b: gcol[:, 2 * EXPERTS * b:2 * EXPERTS * b + P], gT_ps)

            def out_T(p):
                pe.wait_ge(y_added, (EXPERTS - 1) * (p + 1))
                take_G(out_ready, p + 1)
                transposes(pG, lambda b: cols_of(yacc, b), oT_ps)

            def first_T(c):
                pe.wait_ge(xn_ready, 2 * c + 1)
                wait(pe, exp_done, UNITS * c)
                transposes(pT0, lambda b: xn[:, b, :], xT_ps)

            def context_T(c):
                pe.wait_ge(c_in, 16 * (c + 1))
                transposes(pT1, lambda b: C[:, b, :], cT_ps)

            def self_queries(c):
                pe.wait_ge(xnT_ready, 2 * c + 1)
                wait(pe, max_done, UNITS * c)
                pe.matmul(pS[:, :], Aqk[:, :], xnT[:, :], start=True, stop=True).then_inc(g_ps, 1)

            def context_keys(c):
                pe.wait_ge(cT_ready, c + 1)
                pe.matmul(pT0[:, :], wkx[:, :], cT[:, :], start=True, stop=True).then_inc(k_ps, 1)

            def self_values(c):
                wait(pe, on_ready, NB * c)
                products(pO, lambda b: cols_of(xnT, b), lambda b: wvs[:, :], vs_ps)

            def body(c, last, experts):
                p = c - 1

                def step(n, between=None, behind=None):
                    if experts:
                        expert_step(p, n, between, behind)
                    else:
                        for products_of in (between, behind):
                            if products_of is not None:
                                products_of()

                pe.wait_ge(gt_ready, c + 1)
                products(pS, lambda b: cols_of(xnT, b), lambda b: cols_of(GT, b), ss_ps)
                products(pT1, lambda b: cols_of(cT, b), lambda b: wvx[:, :], vx_ps)
                if second_on(c):
                    out_T(c - 2)
                step(0)

                def stack(hi_sel, lo_sel, g, done):
                    bank = pT[g % 2]
                    pe.matmul(bank[:, :], hi_sel[:, g, :], qk_hi[:, :], start=True, stop=False)
                    pe.matmul(bank[:, :], lo_sel[:, g, :], qk_lo[:, :], start=False, stop=True).then_inc(done, 1)

                step(1)
                pe.wait_ge(qklo_ready, 2 * c + 1)
                stack(k_hi_sel, k_lo_sel, 0, kst_ps)
                pe.wait_ge(vx_ready, c + 1)
                stack(k_hi_sel, k_lo_sel, 1, kst_ps)
                step(2)
                pe.wait_ge(kst_a, 2 * c + 1)
                stack(k_hi_sel, k_lo_sel, 2, kst_ps)
                pe.wait_ge(kst_d, 2 * c + 1)
                stack(k_hi_sel, k_lo_sel, 3, kst_ps)
                pe.wait_ge(p_ready, c + 1)
                pe.wait_ge(vs_ready, c + 1)
                transposes(pO, lambda b: cols_of(Ps, b), pt_ps)
                if experts:
                    gates_T(p)
                step(3)
                pe.wait_ge(pts_ready, c + 1)
                products(pS, lambda b: PTs[:, b, :], lambda b: Vs[:, b, :], pvs_ps)
                for n in range(4, 9):
                    step(n)
                pe.wait_ge(xn_ready, 2 * c + 2)
                transposes(pO, lambda b: xn[:, b, :], xT_ps)

                def queries():
                    pe.wait_ge(xnT_ready, 2 * c + 2)
                    pe.wait_ge(kst_a, 2 * c + 2)
                    pe.matmul(pT0[:, :], wqx[:, :], xnT[:, :], start=True, stop=True).then_inc(q_ps, 1)

                step(9, behind=queries)
                step(10)

                def first_stacks():
                    pe.wait_ge(qklo_ready, 2 * c + 2)
                    stack(q_hi_sel, q_lo_sel, 0, qst_ps)
                    pe.wait_ge(kst_d, 2 * c + 2)
                    stack(q_hi_sel, q_lo_sel, 1, qst_ps)

                step(11, first_stacks)
                pe.wait_ge(qst_a, 2 * c + 1)
                stack(q_hi_sel, q_lo_sel, 2, qst_ps)
                pe.wait_ge(qst_d, 2 * c + 1)
                stack(q_hi_sel, q_lo_sel, 3, qst_ps)

                def scores(t):
                    b, g = divmod(t, GROUPS)
                    if g == 0:
                        pe.wait_ge(kbd_in[b % 2], 16 * HPG * (2 * c + b // 2 + 1))
                    if t == 0:
                        pe.wait_ge(x1_done, c + 1)
                    if t < GROUPS:
                        pe.wait_ge((qst_a, qst_d)[g % 2], 2 * c + 1 + g // 2)
                    bank = pO if t in SECOND_BANK else pS
                    wait(pe, max_done, UNITS * c + (t if t >= AHEAD else max(t - 1, 0)))
                    pe.matmul(bank[:, :], Qst[:, g, b * P:(b + 1) * P],
                              Kbd[:, b % 2, g, :, :].rearrange("p h k -> p (h k)"), start=True, stop=False)
                    pe.matmul(tiles(bank), identb[:, :], maskb[:, :].unsqueeze(1).to_broadcast([P, HPG, P]),
                              start=False, stop=True).then_inc(s_ps, 1)

                def maxima_T(b):
                    pe.wait_ge(mcol_ready, NB * c + b + 1)
                    take_G(mT_ready, NB * c + b + 1)
                    pe.transpose(pG[0:2 * HEADS, 0:P], mcol[:, :, :, :].rearrange("p j s g -> p (j s g)"),
                                 identf[:, :]).then_inc(mT_ps, 1)

                def scores_T(u):
                    b, g = divmod(u, GROUPS)
                    if g == 0:
                        pe.wait_ge(m_in, 16 * HPG * (NB * c + b + 1))
                        pe.wait_ge(qbd_in[b % 2], 16 * HPG * (2 * c + b // 2 + 1))
                    wait(pe, exp_done, UNITS * c + u - 1)
                    bank = pT[u % 2]
                    pe.matmul(bank[:, :], Kst[:, g, b * P:(b + 1) * P],
                              Qbd[:, b % 2, g, :, :].rearrange("p h q -> p (h q)"), start=True,
                              stop=True).then_inc(st_ps, 1)

                def values(u):
                    b, g = divmod(u, GROUPS)
                    pe.wait_ge(keep_done, UNITS * c + u + 1)
                    if g == 0:
                        pe.wait_ge(vpad_ready, NB * c + b + 1)
                        if b == 0:
                            pe.wait_ge(max_done, UNITS * c + SECOND_BANK[-1] + 1)
                        wait(pe, on_ready, NB * c + b)
                    for j in range(HPG):
                        h = HPG * g + j
                        half = h // 8
                        mm = pe.matmul(cols_of(pO, half), PT[:, u % 2, j * P:(j + 1) * P],
                                       Vpad[:, b % 2, h, :], start=(h % 8 == 0), stop=(h % 8 == 7))
                    mm.then_inc(pv_ps, 1)

                def o_T(b):
                    pe.wait_ge(on_ready, NB * c + b + 1)
                    take_G(ot_ready, NB * c + b + 1)
                    pe.transpose(pG[:, 0:P], On[:, :], identf[:, :]).then_inc(ot_ps, 1)

                def project(b):
                    take_G(x2_done, NB * c + b + 1)
                    pe.matmul(pG[:, 0:P], OT[:, :], wo[:, :], start=True, stop=True).then_inc(wo_ps, 1)

                def third_T(b):
                    pe.wait_ge(x3n_ready, NB * c + b + 1)
                    take_G(x3T_ready, NB * c + b + 1)
                    pe.transpose(pG[:, 0:P], x3n[:, :], identf[:, :]).then_inc(x3T_ps, 1)

                scores(0)
                scores(1)
                step(12)
                scores(2)
                step(13, lambda: scores(3))
                scores(4)
                step(14, lambda: maxima_T(0))
                scores(5)
                step(15)
                scores(6)
                step(16)
                for u in range(UNITS):
                    b, g = divmod(u, GROUPS)
                    scores_T(u)
                    if u < UNITS - AHEAD:
                        scores(u + AHEAD)
                    if g == 1 and b + 1 < NB:
                        maxima_T(b + 1)
                    if g == 0 and b >= 2:
                        third_T(b - 2)

                    def between():
                        if g == 1 and b >= 1:
                            o_T(b - 1)
                        if u >= 1:
                            values(u - 1)

                    if step_of(u):
                        step(step_of(u), between)
                    else:
                        between()
                    if g == 1 and b >= 1:
                        project(b - 1)

                def between():
                    values(UNITS - 1)
                    third_T(NB - 2)

                def behind():
                    o_T(NB - 1)
                    if not last:
                        first_T(c + 1)

                step(31, between, behind)
                step(32)
                project(NB - 1)
                if not last:
                    context_T(c + 1)
                step(33)
                if not last:
                    self_queries(c + 1)
                    self_values(c + 1)
                third_T(NB - 1)
                if not last:
                    context_keys(c + 1)
                pe.wait_ge(x3T_ready, NB * (c + 1))
                take_G(lg_copied, c + 1)
                for b in range(NB):
                    mm = pe.matmul(pG[:, b * EXPERTS:(b + 1) * EXPERTS], cols_of(x3T, b), gw[:, :],
                                   start=True, stop=True)
                mm.then_inc(lg_ps, 1)

            pe.wait_ge(ident_ready, 1)
            pe.wait_ge(qk_in, 16 * 2)
            pe.wait_ge(rows_in, 16 * 5)
            for i in range(3):
                mm = pe.transpose(cols_of(pH0, i), Gb[:, 0, i * P:(i + 1) * P], identf[:, :])
            mm.then_inc(setup_T, 1)
            pe.wait_ge(setup_cp, 1)
            pe.matmul(pH1[:, 0:P], Gb[:, 1, P:2 * P], Gb[:, 1, 2 * P:3 * P], start=True,
                      stop=True).then_inc(aqk_ps, 1)
            first_T(0)
            context_T(0)
            pe.wait_ge(aqk_ready, 1)
            self_queries(0)
            pe.wait_ge(wts_in, 16 * 7)
            self_values(0)
            context_keys(0)
            pe.wait_ge(cast_done, 1)
            body(0, False, False)
            pe.wait_ge(w_lo, 2 * EXPERTS)
            body(1, False, True)
            with pe.Fori(2, CHUNKS - 1) as c:
                last_G[0], last_G[1] = lg_copied, c
                body(c, False, True)
            last_G[0], last_G[1] = lg_copied, CHUNKS - 1
            body(CHUNKS - 1, True, True)
            out_T(CHUNKS - 2)
            for n in range(STEPS + LAG):
                if n == GATES_STEP:
                    gates_T(CHUNKS - 1)
                expert_step(CHUNKS - 1, n)
            out_T(CHUNKS - 1)


_INS = ['x', 'ctx_1024', 'L0_attn_W_query', 'L0_attn_W_key', 'L0_attn_W_value', 'L0_xattn_w_q', 'L0_xattn_b_q',
        'L0_xattn_w_k', 'L0_xattn_b_k', 'L0_xattn_w_v', 'L0_xattn_b_v', 'L0_xattn_w_o', 'L0_xattn_b_o',
        'L0_ffn_gate_w', 'L0_ffn_w1', 'L0_ffn_b1', 'L0_ffn_w2', 'L0_ffn_b2']


def kernel(**inputs):
    import numpy as _np
    import concourse.bacc as _bacc
    from concourse import mybir as _mybir
    from concourse.bass_utils import run_bass_kernel_spmd as _run

    nc = _bacc.Bacc("TRN2", target_bir_lowering=False, num_devices=1)
    arrays, args = {}, []
    for name in _INS:
        a = _np.ascontiguousarray(inputs[name])
        arrays[f"in_{name}_dram"] = a
        args.append(nc.dram_tensor(f"in_{name}_dram", a.shape, _mybir.dt.from_np(a.dtype), kind="ExternalInput").ap())
    out = nc.dram_tensor("out_0_dram", inputs['x'].shape, _mybir.dt.float32, kind="ExternalOutput").ap()
    decoder_layer(nc, *args, out)
    r = _run(nc, [arrays], core_ids=[0])
    return r.results[0]["out_0_dram"]
```
